# Optimizing a Trainium2 kernel written in Bass

```python
import numpy as np
import jax
import jax.numpy as jnp

def _softmax(x, axis=-1):
    return jax.nn.softmax(x, axis=axis)

def _gelu(x):
    return jax.nn.gelu(x, approximate=True)

def _silu(x):
    return jax.nn.silu(x)

def _sigmoid(x):
    return jax.nn.sigmoid(x)

def _layernorm(x, axis=-1, eps=1e-05):
    m = jnp.mean(x, axis=axis, keepdims=True)
    v = jnp.var(x, axis=axis, keepdims=True)
    return (x - m) / jnp.sqrt(v + eps)

def _scatter_add(tgt, idx, src, axis=0):
    return tgt.at[idx].add(src)

def _segment_sum(src, seg, n):
    return jax.ops.segment_sum(src, seg, n)
kernel_name = 'mk_gnn_preln_d2_gnn_r8_10aee3'

def setup_inputs(seed: int=0):
    np.random.seed(seed)
    _w = jnp.asarray

    def _rec_inputs():
        import jax
        import jax.numpy as jnp
        _gk = jax.random.key(seed)
        x = -0.000202 + 1 * jax.random.normal(jax.random.fold_in(_gk, 1), (6250, 160), jnp.float32)
        _s = jax.random.randint(jax.random.fold_in(_gk, 2), (50000,), 0, 6250, jnp.int32)
        _d = jax.random.randint(jax.random.fold_in(_gk, 3), (50000,), 0, 6250, jnp.int32)
        _loop = jnp.arange(6250, dtype=jnp.int32)
        src = jnp.concatenate([_s, _d, _loop])
        dst = jnp.concatenate([_d, _s, _loop])
        _o = jnp.argsort(dst, stable=True)
        src = src[_o]
        dst = dst[_o]
        edge_attr_4 = 0.0012443 + 1.0001 * jax.random.normal(jax.random.fold_in(_gk, 12), (106250, 4), jnp.float32)
        edge_attr_64 = 0.000127647 + 1.00004 * jax.random.normal(jax.random.fold_in(_gk, 13), (106250, 64), jnp.float32)
        node_vec1 = jax.random.uniform(jax.random.fold_in(_gk, 15), (6250, 1), jnp.float32, 0.0, 1)
        return (x, src, dst, edge_attr_4, edge_attr_64, node_vec1)
    x, src, dst, edge_attr_4, edge_attr_64, node_vec1 = _rec_inputs()

    def _L0_gnn_setup():
        import jax, jax.numpy as jnp
        import numpy as np
        N, E = (5000, 80000)
        S_IN, V_IN = (64, 32)
        S_MID, V_MID = (96, 128)
        S_OUT, V_OUT = (96, 32)
        R = 64
        FC_HID = 64
        W_NUMEL = 64 + 64 + 32 + 32 + 32
        NUM_NEIGHBORS = 16.0

        def _inv(d):
            return 1.0 / jnp.sqrt(jnp.float32(d))

        def _forward(node_features, node_attr, edge_attr, edge_scalars, lin1_ws, lin1_wv, fc_w1, fc_w2, sc_ws, sc_wv, lin2_ws, lin2_wv, edge_src, edge_dst):
            n = node_features.shape[0]
            s = node_features[:, :S_IN]
            v = node_features[:, S_IN:].reshape(n, V_IN, 3)
            a = node_attr
            sc_s = s @ sc_ws * a * _inv(S_IN)
            sc_v = jnp.einsum('nci,cd->ndi', v, sc_wv) * a[:, :, None] * _inv(V_IN)
            h_s = s @ lin1_ws * a * _inv(S_IN)
            h_v = jnp.einsum('nci,cd->ndi', v, lin1_wv) * a[:, :, None] * _inv(V_IN)
            hid = jax.nn.silu(edge_scalars @ fc_w1 * _inv(R))
            w = hid @ fc_w2 * _inv(FC_HID)
            w1, w2, w3, w4, w5 = jnp.split(w, [64, 128, 160, 192], axis=-1)
            es = h_s[edge_src]
            ev = h_v[edge_src]
            e0 = edge_attr[:, :1]
            e1 = edge_attr[:, 1:4]
            m_s1 = w1 * es * e0
            m_s2 = w4 * jnp.einsum('eci,ei->ec', ev, e1) * _inv(3)
            m_v1 = (w2 * es)[:, :, None] * e1[:, None, :]
            m_v2 = w3[:, :, None] * ev * e0[:, :, None]
            m_v3 = w5[:, :, None] * jnp.cross(ev, e1[:, None, :]) * _inv(2)
            mid_s = jnp.concatenate([m_s1, m_s2], axis=-1)
            mid_v = jnp.concatenate([m_v1, m_v2, m_v3], axis=1)
            inv_nn = 1.0 / jnp.sqrt(jnp.float32(NUM_NEIGHBORS))
            agg_s = jax.ops.segment_sum(mid_s, edge_dst, num_segments=n) * inv_nn
            agg_v = jax.ops.segment_sum(mid_v, edge_dst, num_segments=n) * inv_nn
            o_s = agg_s @ lin2_ws * a * _inv(S_MID)
            o_v = jnp.einsum('nci,cd->ndi', agg_v, lin2_wv) * a[:, :, None] * _inv(V_MID)
            pre_s = sc_s + o_s
            pre_v = sc_v + o_v
            scalars = jax.nn.silu(pre_s[:, :64])
            gates = jax.nn.sigmoid(pre_s[:, 64:96])
            gated = gates[:, :, None] * pre_v
            return jnp.concatenate([scalars, gated.reshape(n, 3 * V_OUT)], axis=-1)
        key = jax.random.key(seed)
        ks = jax.random.split(key, 13)
        return {'node_features': jax.random.normal(ks[0], (N, S_IN + 3 * V_IN), jnp.float32), 'node_attr': jnp.ones((N, 1), jnp.float32), 'edge_src': jax.random.randint(ks[1], (E,), 0, N), 'edge_dst': jax.random.randint(ks[2], (E,), 0, N), 'edge_attr': jax.random.normal(ks[3], (E, 4), jnp.float32), 'edge_scalars': jax.random.normal(ks[4], (E, R), jnp.float32), 'lin1_ws': jax.random.normal(ks[5], (S_IN, S_IN), jnp.float32), 'lin1_wv': jax.random.normal(ks[6], (V_IN, V_IN), jnp.float32), 'fc_w1': jax.random.normal(ks[7], (R, FC_HID), jnp.float32), 'fc_w2': jax.random.normal(ks[8], (FC_HID, W_NUMEL), jnp.float32), 'sc_ws': jax.random.normal(ks[9], (S_IN, S_OUT), jnp.float32), 'sc_wv': jax.random.normal(ks[10], (V_IN, V_OUT), jnp.float32), 'lin2_ws': jax.random.normal(ks[11], (S_MID, S_OUT), jnp.float32), 'lin2_wv': jax.random.normal(ks[12], (V_MID, V_OUT), jnp.float32)}
    _L0_gnn_all = _L0_gnn_setup()
    _L0_gnn_in = {k: v for k, v in _L0_gnn_all.items() if k in ('lin1_ws', 'lin1_wv', 'fc_w1', 'fc_w2', 'sc_ws', 'sc_wv', 'lin2_ws', 'lin2_wv')}
    del _L0_gnn_all

    def _L1_gnn_setup():
        import jax, jax.numpy as jnp
        import numpy as np
        N = 2500
        E = 80000
        INV_SQRT3 = 0.5773502691896258
        INV8 = 0.125
        INV_SQRT32 = 0.17677669529663687
        INV64 = 0.015625
        INV32 = 0.03125
        INV_SQRT2048 = 0.022097086912079608
        key = jax.random.key(seed)
        ks = jax.random.split(key, 16)
        f32 = jnp.float32
        return {'node_features': jax.random.normal(ks[0], (N, 160), f32), 'edge_index': jax.random.randint(ks[1], (2, E), 0, N), 'edge_attr_tensor': jax.random.normal(ks[2], (E, 4), f32), 'node_attr_scalar_raw': jax.random.normal(ks[3], (N, 1), f32), 'Wm_ss': jax.random.normal(ks[4], (64, 64), f32), 'Wm_vv': jax.random.normal(ks[5], (32, 64), f32), 'Wm_sv': jax.random.normal(ks[6], (64, 32), f32), 'Wm_vs': jax.random.normal(ks[7], (32, 32), f32), 'Lm_s': jax.random.normal(ks[8], (64, 64), f32), 'Lm_v': jax.random.normal(ks[9], (32, 32), f32), 'Wu_ss': jax.random.normal(ks[10], (64, 64, 64), f32), 'Wu_vv': jax.random.normal(ks[11], (32, 32, 64), f32), 'Wu_sv': jax.random.normal(ks[12], (64, 32, 32), f32), 'Wu_vs': jax.random.normal(ks[13], (32, 64, 32), f32), 'Lu_s': jax.random.normal(ks[14], (64, 64), f32), 'Lu_v': jax.random.normal(ks[15], (32, 32), f32)}
    _L1_gnn_all = _L1_gnn_setup()
    _L1_gnn_in = {k: v for k, v in _L1_gnn_all.items() if k in ('Wm_ss', 'Wm_vv', 'Wm_sv', 'Wm_vs', 'Lm_s', 'Lm_v', 'Wu_ss', 'Wu_vv', 'Wu_sv', 'Wu_vs', 'Lu_s', 'Lu_v')}
    del _L1_gnn_all
    return {'x': x, 'src': src, 'dst': dst, 'edge_attr_4': edge_attr_4, 'edge_attr_64': edge_attr_64, 'node_vec1': node_vec1, 'L0_gnn_lin1_ws': _L0_gnn_in['lin1_ws'], 'L0_gnn_lin1_wv': _L0_gnn_in['lin1_wv'], 'L0_gnn_fc_w1': _L0_gnn_in['fc_w1'], 'L0_gnn_fc_w2': _L0_gnn_in['fc_w2'], 'L0_gnn_sc_ws': _L0_gnn_in['sc_ws'], 'L0_gnn_sc_wv': _L0_gnn_in['sc_wv'], 'L0_gnn_lin2_ws': _L0_gnn_in['lin2_ws'], 'L0_gnn_lin2_wv': _L0_gnn_in['lin2_wv'], 'L1_gnn_Wm_ss': _L1_gnn_in['Wm_ss'], 'L1_gnn_Wm_vv': _L1_gnn_in['Wm_vv'], 'L1_gnn_Wm_sv': _L1_gnn_in['Wm_sv'], 'L1_gnn_Wm_vs': _L1_gnn_in['Wm_vs'], 'L1_gnn_Lm_s': _L1_gnn_in['Lm_s'], 'L1_gnn_Lm_v': _L1_gnn_in['Lm_v'], 'L1_gnn_Wu_ss': _L1_gnn_in['Wu_ss'], 'L1_gnn_Wu_vv': _L1_gnn_in['Wu_vv'], 'L1_gnn_Wu_sv': _L1_gnn_in['Wu_sv'], 'L1_gnn_Wu_vs': _L1_gnn_in['Wu_vs'], 'L1_gnn_Lu_s': _L1_gnn_in['Lu_s'], 'L1_gnn_Lu_v': _L1_gnn_in['Lu_v']}

def reference(x, src, dst, edge_attr_4, edge_attr_64, node_vec1, L0_gnn_lin1_ws, L0_gnn_lin1_wv, L0_gnn_fc_w1, L0_gnn_fc_w2, L0_gnn_sc_ws, L0_gnn_sc_wv, L0_gnn_lin2_ws, L0_gnn_lin2_wv, L1_gnn_Wm_ss, L1_gnn_Wm_vv, L1_gnn_Wm_sv, L1_gnn_Wm_vs, L1_gnn_Lm_s, L1_gnn_Lm_v, L1_gnn_Wu_ss, L1_gnn_Wu_vv, L1_gnn_Wu_sv, L1_gnn_Wu_vs, L1_gnn_Lu_s, L1_gnn_Lu_v):
    import jax
    import jax.numpy as jnp

    def _L0_gnn_ref(node_features, node_attr, edge_src, edge_dst, edge_attr, edge_scalars, lin1_ws, lin1_wv, fc_w1, fc_w2, sc_ws, sc_wv, lin2_ws, lin2_wv):
        import jax, jax.numpy as jnp
        import numpy as np
        N, E = (5000, 80000)
        S_IN, V_IN = (64, 32)
        S_MID, V_MID = (96, 128)
        S_OUT, V_OUT = (96, 32)
        R = 64
        FC_HID = 64
        W_NUMEL = 64 + 64 + 32 + 32 + 32
        NUM_NEIGHBORS = 16.0

        def _inv(d):
            return 1.0 / jnp.sqrt(jnp.float32(d))

        def _forward(node_features, node_attr, edge_attr, edge_scalars, lin1_ws, lin1_wv, fc_w1, fc_w2, sc_ws, sc_wv, lin2_ws, lin2_wv, edge_src, edge_dst):
            n = node_features.shape[0]
            s = node_features[:, :S_IN]
            v = node_features[:, S_IN:].reshape(n, V_IN, 3)
            a = node_attr
            sc_s = s @ sc_ws * a * _inv(S_IN)
            sc_v = jnp.einsum('nci,cd->ndi', v, sc_wv) * a[:, :, None] * _inv(V_IN)
            h_s = s @ lin1_ws * a * _inv(S_IN)
            h_v = jnp.einsum('nci,cd->ndi', v, lin1_wv) * a[:, :, None] * _inv(V_IN)
            hid = jax.nn.silu(edge_scalars @ fc_w1 * _inv(R))
            w = hid @ fc_w2 * _inv(FC_HID)
            w1, w2, w3, w4, w5 = jnp.split(w, [64, 128, 160, 192], axis=-1)
            es = h_s[edge_src]
            ev = h_v[edge_src]
            e0 = edge_attr[:, :1]
            e1 = edge_attr[:, 1:4]
            m_s1 = w1 * es * e0
            m_s2 = w4 * jnp.einsum('eci,ei->ec', ev, e1) * _inv(3)
            m_v1 = (w2 * es)[:, :, None] * e1[:, None, :]
            m_v2 = w3[:, :, None] * ev * e0[:, :, None]
            m_v3 = w5[:, :, None] * jnp.cross(ev, e1[:, None, :]) * _inv(2)
            mid_s = jnp.concatenate([m_s1, m_s2], axis=-1)
            mid_v = jnp.concatenate([m_v1, m_v2, m_v3], axis=1)
            inv_nn = 1.0 / jnp.sqrt(jnp.float32(NUM_NEIGHBORS))
            agg_s = jax.ops.segment_sum(mid_s, edge_dst, num_segments=n) * inv_nn
            agg_v = jax.ops.segment_sum(mid_v, edge_dst, num_segments=n) * inv_nn
            o_s = agg_s @ lin2_ws * a * _inv(S_MID)
            o_v = jnp.einsum('nci,cd->ndi', agg_v, lin2_wv) * a[:, :, None] * _inv(V_MID)
            pre_s = sc_s + o_s
            pre_v = sc_v + o_v
            scalars = jax.nn.silu(pre_s[:, :64])
            gates = jax.nn.sigmoid(pre_s[:, 64:96])
            gated = gates[:, :, None] * pre_v
            return jnp.concatenate([scalars, gated.reshape(n, 3 * V_OUT)], axis=-1)
        return _forward(node_features, node_attr, edge_attr, edge_scalars, lin1_ws, lin1_wv, fc_w1, fc_w2, sc_ws, sc_wv, lin2_ws, lin2_wv, edge_src, edge_dst)

    def _L1_gnn_ref(node_features, edge_index, edge_attr_tensor, node_attr_scalar_raw, Wm_ss, Wm_vv, Wm_sv, Wm_vs, Lm_s, Lm_v, Wu_ss, Wu_vv, Wu_sv, Wu_vs, Lu_s, Lu_v):
        import jax, jax.numpy as jnp
        import numpy as np
        N = 2500
        E = 80000
        INV_SQRT3 = 0.5773502691896258
        INV8 = 0.125
        INV_SQRT32 = 0.17677669529663687
        INV64 = 0.015625
        INV32 = 0.03125
        INV_SQRT2048 = 0.022097086912079608
        n = node_features.shape[0]
        e = edge_attr_tensor.shape[0]
        row, col = (edge_index[0], edge_index[1])
        r_vec = edge_attr_tensor[:, :3]
        dist = edge_attr_tensor[:, 3:4]
        xj = node_features[col]
        s = xj[:, :64]
        v = xj[:, 64:].reshape(e, 32, 3)
        m0 = s @ Wm_ss * dist * INV8 + jnp.einsum('eui,ei->eu', v, r_vec) @ Wm_vv * (INV_SQRT3 * INV_SQRT32)
        m1 = (s @ Wm_sv)[:, :, None] * r_vec[:, None, :] * INV8 + jnp.einsum('eui,uw->ewi', v, Wm_vs) * dist[:, :, None] * INV_SQRT32
        m0 = m0 + s @ Lm_s * INV8
        m1 = m1 + jnp.einsum('eui,uw->ewi', v, Lm_v) * INV_SQRT32
        msg = jnp.concatenate([m0, m1.reshape(e, 96)], axis=-1)
        agg = jax.ops.segment_sum(msg, row, num_segments=n)
        a0 = agg[:, :64]
        a1 = agg[:, 64:].reshape(n, 32, 3)
        xs = node_features[:, :64]
        xv = node_features[:, 64:].reshape(n, 32, 3)
        u0 = jnp.einsum('nu,nv,uvw->nw', xs, a0, Wu_ss) * INV64 + jnp.einsum('nui,nvi,uvw->nw', xv, a1, Wu_vv) * (INV_SQRT3 * INV32)
        u1 = jnp.einsum('nu,nvi,uvw->nwi', xs, a1, Wu_sv) * INV_SQRT2048 + jnp.einsum('nui,nv,uvw->nwi', xv, a0, Wu_vs) * INV_SQRT2048
        u0 = u0 + xs @ Lu_s * INV8
        u1 = u1 + jnp.einsum('nui,uw->nwi', xv, Lu_v) * INV_SQRT32
        upd = jnp.concatenate([u0, u1.reshape(n, 96)], axis=-1)
        return node_features + upd
    edge_index = jnp.stack([src, dst])
    h = jnp.maximum(_layernorm(x, axis=-1), 0.0)
    x = x + _L0_gnn_ref(h, node_vec1, src, dst, edge_attr_4, edge_attr_64, L0_gnn_lin1_ws, L0_gnn_lin1_wv, L0_gnn_fc_w1, L0_gnn_fc_w2, L0_gnn_sc_ws, L0_gnn_sc_wv, L0_gnn_lin2_ws, L0_gnn_lin2_wv)
    h = jnp.maximum(_layernorm(x, axis=-1), 0.0)
    x = x + _L1_gnn_ref(h, edge_index, edge_attr_4, node_vec1, L1_gnn_Wm_ss, L1_gnn_Wm_vv, L1_gnn_Wm_sv, L1_gnn_Wm_vs, L1_gnn_Lm_s, L1_gnn_Lm_v, L1_gnn_Wu_ss, L1_gnn_Wu_vv, L1_gnn_Wu_sv, L1_gnn_Wu_vs, L1_gnn_Lu_s, L1_gnn_Lu_v)
    return x

_drawn_inputs = setup_inputs


def setup_inputs(seed=0):
    import zlib

    import numpy as np

    out = dict(_drawn_inputs(seed))
    spreads = {}
    factors = {}
    for name, (base, spread) in spreads.items():
        noise = np.random.default_rng([zlib.crc32(name.encode()), seed]).standard_normal(out[name].shape)
        drawn = base * np.exp(spread * noise) if base else spread * noise
        out[name] = jnp.asarray(drawn.astype(out[name].dtype))
    for name, factor in factors.items():
        out[name] = (out[name] * factor).astype(out[name].dtype)
    return out
```

```python
from contextlib import ExitStack

import concourse.bass as bass
from concourse import mybir

F32 = mybir.dt.float32
BF16 = mybir.dt.bfloat16
I32 = mybir.dt.int32
ALU = mybir.AluOpType
ACT = mybir.ActivationFunctionType
AX = mybir.AxisListType
ds = bass.ds

TE = 125
S, V = 64, 32
C = S + 3 * V
W5 = 2 * S + 3 * V
MSG = 2 * S + 9 * V
PRE = S + V + 3 * V
G = 5
BT = 2 * G
PAIRS = BT // 2
WIN = 16
GWIN = 64
MAPS = 5
MSG_BANKS = 5
TABLES = G
CB = 5
HIDA, HIDB = 3 * TE, 2 * TE
NC = 2 * TE
EPS = 1e-5

K_S0 = 0.125 * 0.25 / 96 ** 0.5
K_V0 = 0.125 * 0.25 / 128 ** 0.5
INV_SQRT3, INV8, INV_SQRT32 = 0.5773502691896258, 0.125, 0.17677669529663687
INV64, INV32, INV_SQRT2048 = 0.015625, 0.03125, 0.022097086912079608


def spread(ap, axis, n):
    ap = ap.unsqueeze(axis)
    shape = list(ap.shape)
    shape[axis] = n
    return ap.to_broadcast(shape)


def others(i):
    return (i + 1) % 3, (i + 2) % 3


class Chain:

    def __init__(self, engine, sem, base=0):
        self.engine, self.sem, self.base, self.n = engine, sem, base, 0

    def step(self, ins):
        self.n += 1
        ins.then_inc(self.sem, 1)

    def wait(self):
        self.engine.wait_ge(self.sem, self.base + self.n)


def build(nc, a):
    N = a["x"].shape[0]
    T = a["src_t"].shape[1]
    NG = T // G
    assert N % (2 * CB * TE) == 0 and (N // NC) % 2 == 1 and T % BT == 0
    passes_max = (N + WIN - 1) // WIN

    SR = -(-(N + TE) // 128) * 128

    def dram(name, shape, dt=F32):
        return nc.dram_tensor(name, shape, dt).ap()

    d = dict(
        table0=dram("table0", [N, C]), own0=dram("own0", [N, PRE]),
        h1=dram("h1_d", [N, C]), kept1=dram("kept1", [N, C]), scalars1_t=dram("scalars1_t", [S, N]),
        maps1=dram("maps1", [N + WIN, MAPS, C]), sums1=[dram(f"sums1_{k}", [SR, C]) for k in range(TABLES)],
        tile_min=dram("tile_min_d", [T]), tile_off=dram("tile_off_d", [T]),
        group_min=dram("group_min_d", [NG]), fast=dram("fast_d", [1]),
        parts_t=dram("parts_t", [96, 5, N], BF16),
    )

    with ExitStack() as top:
        def sb(ctx, name, shape, dt=F32):
            return ctx.enter_context(nc.sbuf_tensor(name, shape, dt))

        def ps(ctx, name, shape, dt=F32):
            return ctx.enter_context(nc.psum_tensor(name, shape, dt))

        def sems(prefix, names):
            return {n: top.enter_context(nc.semaphore(prefix + n)) for n in names.split()}

        s = sems("edge_", "based idx_set mark es_a es_b hid_mm hid_act w_mm products onehots "
                          "scattered evacuated folded mapped added chain src_rows0 src_rows1 turned turned_out "
                          "msg_mm msg_out")
        s["window"] = [top.enter_context(nc.semaphore(f"edge_window{t}")) for t in range(BT)]
        s["gathered"] = [top.enter_context(nc.semaphore(f"edge_gathered{t}")) for t in range(BT)]
        numbers = sorted(x.num for v in s.values() for x in (v if isinstance(v, list) else [v]))
        edge_sems = range(numbers[0], numbers[-1] + 1)
        assert len(edge_sems) == len(numbers)

        ident = sb(top, "ident", [128, 128])
        ident_b = sb(top, "ident_b", [128, 128], BF16)
        zeros_b = sb(top, "zeros_b", [128, 512], BF16)

        with ExitStack() as edges:
            agg_t = sb(edges, "agg_t", [96, 2, N + GWIN])
            n_pass = sb(edges, "n_pass", [1, 1], I32)
            e = dict(
                src_i=sb(edges, "src_i", [TE, T], I32), dst_f=sb(edges, "dst_f", [TE, T]),
                attr=sb(edges, "attr", [TE, T, 4]), tile_min=sb(edges, "tile_min", [TE, T]),
                dst_rel=sb(edges, "dst_rel", [TE, T]), tile_off=sb(edges, "tile_off", [1, T]),
                group_min=sb(edges, "group_min", [1, NG]), group_min_now=sb(edges, "group_min_now", [1, NG]),
                packed_off=sb(edges, "packed_off", [1, NG], I32), packed_parts=sb(edges, "packed_parts", [1, 2, NG], I32),
                tile_off_i=sb(edges, "tile_off_i", [1, T], I32),
                group_base_i=sb(edges, "group_base_i", [1, NG + 1], I32),
                fast=sb(edges, "fast", [128, 1]), pass_base=sb(edges, "pass_base", [128, 1]),
                slots=sb(edges, "slots", [TE, WIN]), idx_now=sb(edges, "idx_now", [TE, 2, G], I32),
                zeros=sb(edges, "zeros", [128, SR // 128 * 20]), zeros_b=zeros_b, agg_t=agg_t,
            )
            setup_stage(nc, a, d, e, sems, ident, ident_b, n_pass, N, T, passes_max)
            project_stage(nc, a, d, sb, ps, sems, ident, N)

            with ExitStack() as layer:
                b = dict(
                    es=sb(layer, "es", [128, HIDA + HIDB]), hid=sb(layer, "hid", [128, HIDA + HIDB]),
                    fc1=sb(layer, "fc1", [128, 128]), fc2=sb(layer, "fc2", [128, 2, W5]),
                    w_s=sb(layer, "w_s", [128, S + V]), w_v=sb(layer, "w_v", [128, V]),
                    gathered=sb(layer, "gathered", [TE, BT, C]), hot=sb(layer, "hot", [TE, 2, G, 5, WIN]),
                    msg=sb(layer, "msg", [TE, BT, MSG]),
                    cross_in=sb(layer, "cross_in", [64, 2, 3, 3, GWIN]),
                    sum_s=sb(layer, "sum_s", [128, 2, GWIN]), sum_v=sb(layer, "sum_v", [128, 2, 3, GWIN]),
                    acc=ps(layer, "acc0", [128, 2, 4, 4, GWIN]), w=ps(layer, "w_ps", [128, 3, 2, 256]),
                    hm=ps(layer, "hid_ps", [128, 512]),
                )
                layer0_start(nc, a, d, sems, b, e)
                passes = nc.values_load(n_pass[0:1, 0:1], min_val=1, max_val=passes_max)
                with nc.Fori(0, passes) as _:
                    layer0_pass(nc, a, d, s, e, b, T)
                    nc.all_engine_barrier(sems_to_clear=edge_sems)

            middle_stage(nc, a, d, sb, ps, sems, ident, ident_b, agg_t, N)

            with ExitStack() as layer:
                b = dict(
                    src_rows=sb(layer, "src_rows", [TE, 2, G, TE], I32), same=sb(layer, "same", [TE, 2, G, TE]),
                    earlier=sb(layer, "earlier", [TE, G, TE]), before=sb(layer, "before", [TE, TE]),
                    spare=sb(layer, "spare", [TE, 1]), double=sb(layer, "double", [TE, G]),
                    shift=sb(layer, "shift", [TE, G]), hot=sb(layer, "hot1", [TE, 2, G, WIN, MAPS]),
                    window=sb(layer, "window", [WIN * MAPS, BT, C]),
                    turned=sb(layer, "turned_sb", [WIN * MAPS, 2, TE]), msg=sb(layer, "msg1", [TE, BT, C]),
                    turned_ps=ps(layer, "turned_ps", [128, 2, 512]), msg_ps=ps(layer, "msg_ps", [128, MSG_BANKS, 512]),
                )
                layer1_start(nc, sems, e, b, N)
                passes = nc.values_load(n_pass[0:1, 0:1], min_val=1, max_val=passes_max)
                with nc.Fori(0, passes) as _:
                    layer1_pass(nc, a, d, s, e, b, T, N)
                    nc.all_engine_barrier(sems_to_clear=edge_sems)

        update_stage(nc, a, d, sb, ps, sems, zeros_b, ident, N)


def setup_stage(nc, a, d, e, sems, ident, ident_b, n_pass, N, T, passes_max):
    q = sems("setup_", "iotas rows loaded chain found worst stored back")
    PG = T // BT
    with ExitStack() as ctx:
        def sb(name, shape, dt=F32):
            return ctx.enter_context(nc.sbuf_tensor(name, shape, dt))

        dst_i, rows_i, rows = sb("dst_i", [TE, T], I32), sb("rows_i", [PG, BT, TE], I32), sb("rows", [PG, BT, TE])
        lo, hi, off, glo = sb("lo", [PG, 2, G]), sb("hi", [PG, 2, G]), sb("off", [PG, 2, G]), sb("glo", [PG, 2])
        misfit, worst, worst_all = sb("misfit", [128, 2, 2, G]), sb("worst", [128, 1]), sb("worst_all", [128, 1])
        fits, passes_f = sb("fits", [128, 1]), sb("passes_f", [1, 1])
        diagonal, slots_i = sb("diagonal", [128, 128], I32), sb("slots_i", [TE, WIN], I32)
        with nc.Block() as block:
            @block.sync
            def _(sp):
                sp.dma_start(rows_i[:, :, :], a["dst"].rearrange("(p t e) -> p t e", p=PG, t=BT)).then_inc(q["rows"], 16)
                sp.dma_start(dst_i[:, :], a["dst_t"]).then_inc(q["loaded"], 16)
                sp.dma_start(e["src_i"][:, :], a["src_t"]).then_inc(q["loaded"], 16)
                sp.dma_start(e["attr"][:, :, :], a["attr_t"]).then_inc(q["loaded"], 16)
                sp.wait_ge(q["found"], 1)
                sp.dma_start(d["tile_min"].rearrange("(p t) -> p t", p=PG),
                             lo[:, :, :].rearrange("p h t -> p (h t)")).then_inc(q["stored"], 16)
                sp.dma_start(d["tile_off"].rearrange("(p t) -> p t", p=PG),
                             off[:, :, :].rearrange("p h t -> p (h t)")).then_inc(q["stored"], 16)
                sp.dma_start(d["group_min"].rearrange("(p h) -> p h", p=PG), glo[:, :]).then_inc(q["stored"], 16)
                sp.dma_start(d["fast"].rearrange("(p o) -> p o", p=1), fits[0:1, :]).then_inc(q["stored"], 16)
                sp.wait_ge(q["stored"], 64)
                sp.dma_start(e["tile_min"][:, :], d["tile_min"].rearrange("(o t) -> o t", o=1).to_broadcast([TE, T])) \
                    .then_inc(q["back"], 16)
                sp.dma_start(e["tile_off"][:, :], d["tile_off"].rearrange("(o t) -> o t", o=1)).then_inc(q["back"], 16)
                sp.dma_start(e["group_min"][:, :], d["group_min"].rearrange("(o t) -> o t", o=1)) \
                    .then_inc(q["back"], 16)
                sp.dma_start(e["fast"][:, :], d["fast"].rearrange("(o t) -> o t", o=1).to_broadcast([128, 1])) \
                    .then_inc(q["back"], 16)
                sp.wait_ge(q["back"], 64)

            @block.gpsimd
            def _(pool):
                pool.iota(diagonal[:, :], [[-1, 128]], base=0, channel_multiplier=1).then_inc(q["iotas"], 1)
                pool.iota(slots_i[:, :], [[1, WIN]], base=0, channel_multiplier=0).then_inc(q["iotas"], 1)
                pool.wait_ge(q["worst"], 1)
                pool.partition_all_reduce(worst_all[:, :], worst[:, :], 128, bass.bass_isa.ReduceOp.max) \
                    .then_inc(q["worst"], 1)

            @block.vector
            def _(dve):
                chain = Chain(dve, q["chain"])
                dve.memset(e["zeros_b"][:, :], 0.0)
                dve.memset(e["zeros"][:, :], 0.0)
                dve.memset(misfit[:, :, :, :], 0.0)
                dve.wait_ge(q["iotas"], 2)
                dve.tensor_scalar(ident[:, :], diagonal[:, :], 0.0, None, ALU.is_equal)
                dve.tensor_scalar(ident_b[:, :], diagonal[:, :], 0.0, None, ALU.is_equal)
                dve.tensor_copy(e["slots"][:, :], slots_i[:, :])
                dve.wait_ge(q["rows"], 16)
                chain.step(dve.tensor_copy(rows[:, :, :], rows_i[:, :, :]))
                chain.wait()
                by_group = rows[:, :, :].rearrange("p (h t) e -> p h t e", h=2)
                dve.tensor_reduce(lo[:, :, :], by_group, AX.X, ALU.min)
                chain.step(dve.tensor_reduce(hi[:, :, :], by_group, AX.X, ALU.max))
                chain.wait()
                chain.step(dve.tensor_reduce(glo[:, :], lo[:, :, :], AX.X, ALU.min))
                chain.wait()
                dve.tensor_tensor(misfit[0:PG, 0, :, :], hi[:, :, :], lo[:, :, :], ALU.subtract)
                chain.step(dve.tensor_tensor(off[:, :, :], lo[:, :, :], spread(glo[:, :], 2, G), ALU.subtract))
                chain.wait()
                dve.tensor_scalar(misfit[0:PG, 0, :, :], misfit[0:PG, 0, :, :], float(WIN - 1), None, ALU.is_gt)
                chain.step(dve.tensor_scalar(misfit[0:PG, 1, :, :], off[:, :, :], float(GWIN - WIN), None, ALU.is_gt))
                chain.wait()
                dve.tensor_reduce(worst[:, :], misfit[:, :, :, :].rearrange("p m h t -> p (m h t)"), AX.X, ALU.max) \
                    .then_inc(q["worst"], 1)
                dve.wait_ge(q["worst"], 2)
                dve.tensor_scalar(fits[:, :], worst_all[:, :], -1.0, 1.0, ALU.mult, ALU.add)
                chain.step(dve.tensor_scalar(passes_f[:, :], worst_all[0:1, :], float(passes_max - 1), 1.0,
                                             ALU.mult, ALU.add))
                chain.wait()
                dve.tensor_copy(n_pass[:, :], passes_f[:, :]).then_inc(q["found"], 1)
                dve.wait_ge(q["loaded"], 48)
                chain.step(dve.tensor_copy(e["dst_f"][:, :], dst_i[:, :]))
                chain.wait()


def normalise(dve, chain, act_sem, sqrt_sem, n_act, x_in, t, x_s, x_v, h):
    chain.wait()
    chain.step(dve.tensor_reduce(t["mean"][:, :], x_in, AX.X, ALU.add))
    chain.wait()
    chain.step(dve.tensor_scalar(t["mean"][:, :], t["mean"][:, :], -1.0 / C, None, ALU.mult))
    chain.wait()
    chain.step(dve.tensor_tensor(t["centred"][:, :, :], x_in, spread(t["mean"][:, :], 2, C), ALU.add))
    chain.wait()
    chain.step(dve.tensor_tensor(t["square"][:, :, :], t["centred"][:, :, :], t["centred"][:, :, :], ALU.mult))
    chain.wait()
    chain.step(dve.tensor_reduce(t["var"][:, :], t["square"][:, :, :], AX.X, ALU.add))
    chain.wait()
    dve.tensor_scalar(t["var"][:, :], t["var"][:, :], 1.0 / C, EPS, ALU.mult, ALU.add).then_inc(act_sem, 1)
    dve.wait_ge(sqrt_sem, n_act)
    chain.step(dve.reciprocal(t["inv"][:, :], t["std"][:, :]))
    chain.wait()
    dve.tensor_tensor(h[:, :, 0:S], x_s, spread(t["inv"][:, :], 2, S), ALU.mult)
    return dve.tensor_tensor(h[:, :, S:C].rearrange("p b (i c) -> p b i c", i=3), x_v,
                             spread(spread(t["inv"][:, :], 2, 3), 3, V), ALU.mult)


def by_component(ap):
    return ap.rearrange("p b (c i) -> p b i c", i=3)


def node_blocks(ap):
    return ap.rearrange("(k b p) f -> p k b f", b=CB, p=TE)


def project_stage(nc, a, d, sb_in, ps_in, sems, ident, N):
    q = sems("proj_", "loaded0 loaded1 weights chain var std normed h turned h_t mm out_a out_v stored0 stored1")
    BODY_BLOCKS = 2 * CB
    BODIES = N // (TE * BODY_BLOCKS)
    with ExitStack() as ctx:
        x = sb_in(ctx, "x_in", [TE, 2, CB, C])
        t = dict(mean=sb_in(ctx, "mean", [TE, CB]), var=sb_in(ctx, "var", [TE, CB]), std=sb_in(ctx, "std", [TE, CB]),
                 inv=sb_in(ctx, "inv", [TE, CB]), centred=sb_in(ctx, "centred", [TE, CB, C]),
                 square=sb_in(ctx, "square", [TE, CB, C]))
        normed = sb_in(ctx, "normed", [TE, 2, CB, C])
        h = sb_in(ctx, "h", [TE, 2, CB, C])
        h_t = sb_in(ctx, "h_t", [96, 2, 2, TE])
        gather_rows = sb_in(ctx, "gather_rows", [TE, 2, CB, C])
        own_rows = sb_in(ctx, "own_rows", [TE, 2, CB, PRE])
        w_s, w_v = sb_in(ctx, "w_s0", [S, S + 96]), sb_in(ctx, "w_v0", [96, 192])
        node_w = sb_in(ctx, "node_w", [TE, N // TE])
        node_s, node_v = sb_in(ctx, "node_s", [TE, N // TE]), sb_in(ctx, "node_v", [TE, N // TE])
        turned = ps_in(ctx, "turned", [128, 2, 4, TE + 3])
        out_s, out_v = ps_in(ctx, "proj_s", [128, 2, 512]), ps_in(ctx, "proj_v", [128, 2, 512])
        x_dram, table_dram, own_dram = node_blocks(a["x"]), node_blocks(d["table0"]), node_blocks(d["own0"])
        loaded, stored = [q["loaded0"], q["loaded1"]], [q["stored0"], q["stored1"]]

        with nc.Block() as block:
            @block.sync
            def _(sp):
                sp.dma_start(w_s[:, :], a["lin_s"]).then_inc(q["weights"], 16)
                sp.dma_start(w_v[:, :], a["lin_v"]).then_inc(q["weights"], 16)
                sp.dma_start(node_w[:, :], a["node_t"]).then_inc(q["weights"], 16)

                def load(k, par):
                    sp.dma_start(x[:, par, :, :], x_dram[:, ds(k, 1), :, :].rearrange("p k b f -> p (k b) f")) \
                        .then_inc(loaded[par], 16)

                def store(k, i, par):
                    sp.wait_ge(q["out_a"], CB * (2 * i + par + 1))
                    sp.wait_ge(q["out_v"], CB * (2 * i + par + 1))
                    sp.dma_start(table_dram[:, ds(k, 1), :, :].rearrange("p k b f -> p (k b) f"),
                                 gather_rows[:, par, :, :]).then_inc(stored[par], 16)
                    sp.dma_start(own_dram[:, ds(k, 1), :, :].rearrange("p k b f -> p (k b) f"),
                                 own_rows[:, par, :, :]).then_inc(stored[par], 16)

                load(0, 0)
                load(1, 1)
                if BODIES > 1:
                    with sp.Fori(0, BODIES - 1) as i:
                        for par in range(2):
                            store(2 * i + par, i, par)
                            load(2 * i + 2 + par, par)
                for par in range(2):
                    store(2 * BODIES - 2 + par, BODIES - 1, par)
                for par in range(2):
                    sp.wait_ge(stored[par], 32 * BODIES)

            @block.vector
            def _(dve):
                dve.wait_ge(q["weights"], 48)
                dve.tensor_scalar(node_s[:, :], node_w[:, :], S ** -0.5, None, ALU.mult)
                dve.tensor_scalar(node_v[:, :], node_w[:, :], V ** -0.5, None, ALU.mult).then_inc(q["weights"], 1)
                dve.wait_ge(q["weights"], 49)
                with dve.Fori(0, BODIES) as i:
                    chain = Chain(dve, q["chain"], 12 * i)
                    for par in range(2):
                        dve.wait_ge(loaded[par], 16 * i + 16)
                        dve.wait_ge(q["h"], 2 * i)
                        last = normalise(dve, chain, q["var"], q["std"], 2 * i + par + 1, x[:, par, :, :], t,
                                         t["centred"][:, :, 0:S], by_component(t["centred"][:, :, S:C]),
                                         normed[:, par, :, :])
                        last.then_inc(q["normed"], 1)
                    for j in range(BODY_BLOCKS):
                        par, b, k = j // CB, j % CB, BODY_BLOCKS * i + j
                        if b == 0:
                            dve.wait_ge(stored[par], 32 * i)
                        dve.wait_ge(q["mm"], k + 1)
                        scale = node_v[:, ds(k, 1)]
                        dve.tensor_scalar(gather_rows[:, par, b, S:C], out_v[0:TE, j % 2, 0:96], scale, None, ALU.mult)
                        dve.tensor_scalar(own_rows[:, par, b, 96:192], out_v[0:TE, j % 2, 96:192], scale, None,
                                          ALU.mult).then_inc(q["out_v"], 1)

            @block.scalar
            def _(act):
                act.wait_ge(q["weights"], 49)
                with act.Fori(0, BODIES) as i:
                    for par in range(2):
                        act.wait_ge(q["var"], 2 * i + par + 1)
                        act.activation(t["std"][:, :], t["var"][:, :], ACT.Sqrt).then_inc(q["std"], 1)
                        act.wait_ge(q["normed"], 2 * i + par + 1)
                        act.wait_ge(q["turned"], 2 * CB * i)
                        act.activation(h[:, par, :, :], normed[:, par, :, :], ACT.Relu).then_inc(q["h"], 1)
                    for j in range(BODY_BLOCKS):
                        par, b, k = j // CB, j % CB, BODY_BLOCKS * i + j
                        act.wait_ge(q["turned"], k + 1)
                        act.activation(h_t[0:S, j % 2, 0, :], turned[0:S, j % 2, 0, 0:TE], ACT.Copy)
                        act.activation(h_t[:, j % 2, 1, :], turned[0:96, j % 2, 1, 0:TE], ACT.Copy).then_inc(q["h_t"], 1)
                        if b == 0:
                            act.wait_ge(stored[par], 32 * i)
                        act.wait_ge(q["mm"], k + 1)
                        scale = node_s[:, ds(k, 1)]
                        act.activation(gather_rows[:, par, b, 0:S], out_s[0:TE, j % 2, 0:S], ACT.Copy, scale=scale)
                        act.activation(own_rows[:, par, b, 0:96], out_s[0:TE, j % 2, S:160], ACT.Copy, scale=scale) \
                            .then_inc(q["out_a"], 1)

            @block.tensor
            def _(pe):
                pe.wait_ge(q["weights"], 48)
                with pe.Fori(0, BODIES) as i:
                    for j in range(BODY_BLOCKS):
                        par, b, k = j // CB, j % CB, BODY_BLOCKS * i + j
                        if b == 0:
                            pe.wait_ge(q["h"], 2 * i + par + 1)
                        pe.transpose(turned[0:96, j % 2, 1, 0:TE], h[:, par, b, S:C], ident[0:TE, 0:TE])
                        pe.transpose(turned[0:S, j % 2, 0, 0:TE], h[:, par, b, 0:S], ident[0:TE, 0:TE]) \
                            .then_inc(q["turned"], 1)
                        pe.wait_ge(q["h_t"], k + 1)
                        if j >= 2:
                            pe.wait_ge(q["out_a"], k - 1)
                            pe.wait_ge(q["out_v"], k - 1)
                        else:
                            pe.wait_ge(q["out_a"], BODY_BLOCKS * i)
                            pe.wait_ge(q["out_v"], BODY_BLOCKS * i)
                        pe.matmul(out_s[0:TE, j % 2, 0:160], h_t[0:S, j % 2, 0, :], w_s[:, :], start=True, stop=True)
                        pe.matmul(out_v[0:TE, j % 2, 0:192], h_t[:, j % 2, 1, :], w_v[:, :], start=True, stop=True) \
                            .then_inc(q["mm"], 1)


def gather_edges(pool, s, e, gathered, table, T, freed):
    with pool.Fori(0, T // BT) as i:
        for g in range(2):
            for k in range(G):
                pool.wait_ge(s["gathered"][G * g + k], 16 * i)
            pool.sem_inc(s["mark"], 1)
            pool.tensor_copy(e["idx_now"][:, g, :], e["src_i"][:, ds(BT * i + G * g, G)]).then_inc(s["idx_set"], 1)
            pool.wait_ge(s["idx_set"], 2 * i + g + 1)
            for k in range(G):
                t = G * g + k
                pool.wait_ge(freed, BT * i + t + 1)
                pool.sem_inc(s["mark"], 1)
                pool.indirect_dma_start(gathered[:, t, :], None, table[:, :],
                                        bass.IndirectOffsetOnAxis(ap=e["idx_now"][:, g, k:k + 1], axis=0)) \
                    .then_inc(s["gathered"][t], 16)
    end_of_pool_dmas(pool, s, T)


def end_of_pool_dmas(pool, s, T):
    for t in range(BT):
        pool.wait_ge(s["gathered"][t], 16 * (T // BT))
    pool.dma_reset(range(s["gathered"][0].num, s["gathered"][-1].num + 1))


def set_windows(dve, chain, s, e, NG):
    base = e["pass_base"]
    chain.step(dve.tensor_scalar(base[:, :], base[:, :], float(WIN), None, ALU.add))
    chain.wait()
    dve.tensor_scalar(e["tile_off_i"][:, :], e["tile_off"][:, :], e["fast"][0:1, :], None, ALU.mult)
    chain.step(dve.tensor_scalar(e["dst_rel"][:, :], e["tile_min"][:, :], base[0:TE, :], e["fast"][0:TE, :],
                                 ALU.subtract, ALU.mult))
    chain.step(dve.tensor_scalar(e["group_min_now"][:, :], e["group_min"][:, :], base[0:1, :], e["fast"][0:1, :],
                                 ALU.subtract, ALU.mult))
    chain.wait()
    dve.memset(e["group_base_i"][:, 0:1], 0)
    dve.tensor_scalar(e["group_base_i"][:, 1:NG + 1], e["group_min_now"][:, :], base[0:1, :], None, ALU.add)
    chain.wait()
    chain.step(dve.scalar_tensor_tensor(e["dst_rel"][:, :], e["dst_f"][:, :], base[0:TE, :], e["dst_rel"][:, :],
                                        ALU.subtract, ALU.subtract))


def pack_offsets(dve, chain, e, NG):
    off = e["tile_off_i"][:, :].rearrange("o (g t) -> o g t", t=G)
    low, high = e["packed_parts"][:, 0, :], e["packed_parts"][:, 1, :]
    chain.wait()
    chain.step(dve.scalar_tensor_tensor(low, off[:, :, 1], 64.0, off[:, :, 0], ALU.mult, ALU.add))
    chain.step(dve.scalar_tensor_tensor(high, off[:, :, 4], 64.0, off[:, :, 3], ALU.mult, ALU.add))
    chain.wait()
    chain.step(dve.scalar_tensor_tensor(low, off[:, :, 2], 64.0 ** 2, low, ALU.mult, ALU.add))
    chain.step(dve.tensor_scalar(high, high, 64.0 ** 3, None, ALU.mult))
    chain.wait()
    chain.step(dve.tensor_tensor(e["packed_off"][:, :], low, high, ALU.bitwise_or))


def make_onehots(dve, chain, s, used, e, hot, i, g):
    now = ds(BT * i + G * g, G)
    dve.wait_ge(used, BT * i + G * g + G)
    chain.step(dve.tensor_tensor(hot[:, g, :, 0, :], spread(e["slots"][:, :], 1, G),
                                 spread(e["dst_rel"][:, now], 2, WIN), ALU.is_equal))
    chain.wait()
    dve.tensor_tensor(hot[:, g, :, 1:5, :], spread(hot[:, g, :, 0, :], 2, 4),
                      spread(e["attr"][:, now, :], 3, WIN), ALU.mult).then_inc(s["onehots"], 1)


def layer0_start(nc, a, d, sems, b, e):
    q = sems("w0_", "loaded scaled")
    cleared = sems("clear_", "cleared")["cleared"]
    with nc.Block() as block:
        @block.sync
        def _(sp):
            sp.dma_start(b["fc1"][:, :], a["fc1"]).then_inc(q["loaded"], 16)
            sp.dma_start(b["fc2"][:, :, :], a["fc2"]).then_inc(q["loaded"], 16)
            sp.dma_start(b["w_s"][:, :], a["lin2_s"]).then_inc(q["loaded"], 16)
            sp.dma_start(b["w_v"][:, :], a["lin2_v"]).then_inc(q["loaded"], 16)

        @block.scalar
        def _(act):
            for table in d["sums1"]:
                act.dma_start(table.rearrange("(p r) f -> p (r f)", p=128).rearrange("p (r f) -> p r f", r=8),
                              spread(e["zeros"][:, :], 1, 8)).then_inc(cleared, 16)
            N = d["h1"].shape[0]
            act.dma_start(d["maps1"][N:N + WIN, :, :], spread(e["zeros"][0:WIN, 0:C], 1, MAPS)).then_inc(cleared, 16)
            act.wait_ge(cleared, 16 * TABLES + 16)

        @block.gpsimd
        def _(pool):
            pool.memset(e["agg_t"][:, 0, :], 0.0).then_inc(q["scaled"], 1)
            pool.wait_ge(q["scaled"], 1)

        @block.vector
        def _(dve):
            dve.memset(e["pass_base"][:, :], -float(WIN))
            dve.memset(e["agg_t"][:, 1, :], 0.0)
            dve.memset(b["sum_s"][:, :, :], 0.0)
            dve.memset(b["sum_v"][:, :, :, :], 0.0)
            dve.memset(b["cross_in"][:, :, :, :, :], 0.0)
            dve.wait_ge(q["loaded"], 64)
            dve.tensor_scalar(b["w_s"][0:V, :], b["w_s"][0:V, :], K_S0 * 3 ** -0.5, None, ALU.mult)
            dve.tensor_scalar(b["w_s"][S:128, :], b["w_s"][S:128, :], K_S0, None, ALU.mult)
            dve.tensor_scalar(b["w_v"][0:96, :], b["w_v"][0:96, :], K_V0, None, ALU.mult)
            dve.tensor_scalar(b["w_v"][96:128, :], b["w_v"][96:128, :], K_V0 * 2 ** -0.5, None, ALU.mult)


def layer0_pass(nc, a, d, s, e, b, T):
    BODIES, NG = T // BT, T // G
    acc, w, hm, hid, es = b["acc"], b["w"], b["hm"], b["hid"], b["es"]
    agg_t, gathered, msg, hot = e["agg_t"], b["gathered"], b["msg"], b["hot"]
    es_dram = a["edge_t"]
    OUT_S, OUT_V = HIDA + 9, HIDA + 9 + GWIN
    part_cols = [(0, 2 * S)] + [(2 * S + 3 * V * i, 3 * V) for i in range(3)]

    with nc.Block() as block:
        @block.sync
        def _(sp):
            def load(k, part):
                lo, n = (0, HIDA) if part == 0 else (HIDA, HIDB)
                sp.dma_start(es[:, lo:lo + n], es_dram[:, ds((HIDA + HIDB) * k + lo, n)]) \
                    .then_inc(s["es_a"] if part == 0 else s["es_b"], 16)

            load(0, 0)
            load(0, 1)
            if BODIES > 1:
                with sp.Fori(0, BODIES - 1) as i:
                    sp.wait_ge(s["hid_mm"], 2 * i + 1)
                    load(i + 1, 0)
                    sp.wait_ge(s["hid_mm"], 2 * i + 2)
                    load(i + 1, 1)
            sp.wait_ge(s["hid_mm"], 2 * BODIES - 1)
            load(BODIES, 0)

        @block.gpsimd
        def _(pool):
            gather_edges(pool, s, e, gathered, d["table0"], T, s["products"])

        @block.vector
        def _(dve):
            chain = Chain(dve, s["based"])
            dve.sem_inc(s["products"], BT)
            dve.sem_inc(s["scattered"], BT)
            set_windows(dve, chain, s, e, NG)
            pack_offsets(dve, chain, e, NG)
            chain.step(dve.memset(b["sum_s"][:, 1, :], 0.0))
            chain.step(dve.memset(b["sum_v"][:, 1, :, :], 0.0))
            chain.step(dve.memset(b["cross_in"][:, 1, :, :, :], 0.0))
            chain.wait()

            def products(i, p):
                dve.wait_ge(s["w_mm"], PAIRS * i + p + 1)
                dve.wait_ge(s["scattered"], BT * i + 2 * p + 2)
                dve.wait_ge(s["gathered"][2 * p], 16 * i + 16)
                dve.wait_ge(s["gathered"][2 * p + 1], 16 * i + 16)
                two = slice(2 * p, 2 * p + 2)
                dve.tensor_tensor(msg[:, two, 0:2 * S].rearrange("p t (w c) -> p t w c", w=2),
                                  w[0:TE, p % 3, :, 0:2 * S].rearrange("p t (w c) -> p t w c", w=2),
                                  spread(gathered[:, two, 0:S], 2, 2), ALU.mult)
                for t in range(2):
                    dve.tensor_tensor(
                        msg[:, 2 * p + t, 2 * S:MSG].rearrange("p (i w c) -> p i w c", i=3, w=3),
                        spread(w[0:TE, p % 3, t, 2 * S:W5].rearrange("p (w c) -> p w c", w=3), 1, 3),
                        spread(gathered[:, 2 * p + t, S:C].rearrange("p (i c) -> p i c", i=3), 2, 3),
                        ALU.mult).then_inc(s["products"], 1)

            def fold_group(count, par, ch):
                dve.wait_ge(s["evacuated"], count + 1)
                src = b["cross_in"]
                ch.step(dve.tensor_tensor(b["sum_s"][0:V, par, :], src[0:V, par, 0, 0, :], src[0:V, par, 1, 1, :],
                                          ALU.add))
                for c in range(3):
                    j, k = others(c)
                    dve.tensor_tensor(b["sum_v"][96:128, par, c, :], src[V:2 * V, par, j, k, :],
                                      src[V:2 * V, par, k, j, :], ALU.subtract)
                ch.wait()
                dve.tensor_tensor(b["sum_s"][0:V, par, :], b["sum_s"][0:V, par, :], src[0:V, par, 2, 2, :],
                                  ALU.add).then_inc(s["folded"], 1)

            def add_group(count):
                dve.wait_ge(s["mapped"], count + 1)
                base = dve.value_load(e["group_base_i"][0:1, ds(count, 1)], min_val=0, max_val=agg_t.shape[2] - GWIN)
                window = agg_t[:, :, ds(base, GWIN)]
                dve.wait_ge(s["added"], count)
                dve.tensor_tensor(window, window, hm[0:96, OUT_S:OUT_S + 2 * GWIN].rearrange("p (k n) -> p k n", k=2),
                                  ALU.add).then_inc(s["added"], 1)

            def body(i, more):
                ch = Chain(dve, s["chain"], 4 * i + 1)
                fold_group(2 * i, 1, ch)
                products(i, 1)
                make_onehots(dve, ch, s, s["scattered"], e, hot, i, 1)
                products(i, 2)
                add_group(2 * i)
                products(i, 3)
                fold_group(2 * i + 1, 0, ch)
                products(i, 4)
                if more:
                    make_onehots(dve, ch, s, s["scattered"], e, hot, i + 1, 0)
                    products(i + 1, 0)
                add_group(2 * i + 1)

            make_onehots(dve, Chain(dve, s["chain"]), s, s["scattered"], e, hot, 0, 0)
            products(0, 0)
            if BODIES > 1:
                with dve.Fori(0, BODIES - 1) as i:
                    body(i, True)
            body(BODIES - 1, False)
            fold_group(NG, 1, Chain(dve, s["chain"], 4 * BODIES))
            add_group(NG)
            dve.wait_ge(s["added"], NG + 1)

        @block.scalar
        def _(act):
            act.sem_inc(s["evacuated"], 1)

            def hidden(n, part, w_before):
                lo, cols = (0, HIDA) if part == 0 else (HIDA, HIDB)
                act.wait_ge(s["hid_mm"], n)
                act.wait_ge(s["w_mm"], w_before)
                act.activation(hid[:, lo:lo + cols], hm[:, 0:cols], ACT.Silu, scale=S ** -0.5) \
                    .then_inc(s["hid_act"], 1)

            def evacuate(i, g):
                act.wait_ge(s["scattered"], BT * i + G * g + G + BT)
                act.wait_ge(s["mapped"], 2 * i + g)
                act.activation(b["sum_v"][0:S, g, :, :], acc[0:S, g, 0, 1:4, :], ACT.Copy)
                act.activation(b["sum_s"][S:128, g, :], acc[S:128, g, 0, 0, :], ACT.Copy)
                act.activation(b["sum_v"][S:96, g, :, :], acc[S:96, g, 1:4, 0, :], ACT.Copy)
                act.activation(b["cross_in"][:, g, :, :, :], acc[0:64, g, 1:4, 1:4, :], ACT.Copy) \
                    .then_inc(s["evacuated"], 1)

            hidden(1, 0, 0)
            with act.Fori(0, BODIES) as i:
                hidden(2 * i + 2, 1, PAIRS * i)
                evacuate(i, 0)
                hidden(2 * i + 3, 0, PAIRS * i + 3)
                evacuate(i, 1)

        @block.tensor
        def _(pe):
            def hidden(n, part, load_sem, k, added):
                lo, cols = (0, HIDA) if part == 0 else (HIDA, HIDB)
                pe.wait_ge(load_sem, 16 * k + 16)
                pe.wait_ge(s["added"], added)
                pe.matmul(hm[:, 0:cols], b["fc1"][:, :], es[:, lo:lo + cols], start=True, stop=True) \
                    .then_inc(s["hid_mm"], 1)

            def weights(p, hid_ready, freed):
                pe.wait_ge(s["hid_act"], hid_ready)
                if freed is not None:
                    pe.wait_ge(s["products"], freed)
                pe.matmul(w[0:TE, p % 3, :, 0:W5], hid[:, TE * p:TE * p + TE], b["fc2"][:, :, :],
                          start=True, stop=True).then_inc(s["w_mm"], 1)

            def begin_group(i, g):
                pe.wait_ge(s["evacuated"], 2 * i + g)
                for half in range(2):
                    pe.matmul(acc[:, g, 2 * half:2 * half + 2, :, :].rearrange("p c k n -> p (c k n)"),
                              e["zeros_b"][:, 0:128], e["zeros_b"][:, :], start=True, stop=False,
                              skip_group_check=True)
                pe.wait_ge(s["onehots"], 2 * i + g + 1)
                packed = pe.value_load(e["packed_off"][0:1, ds(2 * i + g, 1)])
                return [nc.s_assert_within(packed // 64 ** k % 64, 0, GWIN - WIN) for k in range(G)]

            def scatter(i, t, off):
                g, k = t // G, t % G
                pe.wait_ge(s["products"], BT * i + t + 1 + BT)
                for c, (col, m) in enumerate(part_cols):
                    mm = pe.matmul(acc[0:m, g, c, :, ds(off, WIN)], msg[:, t, col:col + m], hot[:, g, k, 1:5, :],
                                   start=False, stop=(k == G - 1), skip_group_check=True)
                mm.then_inc(s["scattered"], 1)

            def map_group(count, par, hid_act):
                pe.wait_ge(s["folded"], count + 1)
                pe.wait_ge(s["hid_act"], hid_act)
                pe.matmul(hm[0:96, OUT_S:OUT_S + GWIN], b["w_s"][:, :], b["sum_s"][:, par, :], start=True, stop=True)
                for c in range(3):
                    mm = pe.matmul(hm[V * c:V * c + V, OUT_V:OUT_V + GWIN], b["w_v"][:, :], b["sum_v"][:, par, c, :],
                                   start=True, stop=True)
                mm.then_inc(s["mapped"], 1)

            pe.wait_ge(s["based"], 12)
            hidden(1, 0, s["es_a"], 0, 0)
            weights(0, 1, None)
            with pe.Fori(0, BODIES) as i:
                next_weights = [
                    (1, 2 * i + 1, BT * i + BT),
                    (2, 2 * i + 1, BT * i + 6),
                    (3, 2 * i + 2, BT * i + BT + 2),
                    (4, 2 * i + 2, BT * i + BT + 4),
                    (0, 2 * i + 3, BT * i + BT + 8),
                ]
                for p in range(PAIRS):
                    weights(*next_weights[p])
                    for t in (2 * p, 2 * p + 1):
                        if t % G == 0:
                            off = begin_group(i, t // G)
                        scatter(i, t, off[t % G])
                        if t == 8:
                            map_group(2 * i + 1, 0, 2 * i + 3)
                    if p == 0:
                        hidden(2 * i + 2, 1, s["es_b"], i, 2 * i)
                    if p == 1:
                        map_group(2 * i, 1, 2 * i + 2)
                    if p == 2:
                        hidden(2 * i + 3, 0, s["es_a"], i + 1, 2 * i + 1)
            map_group(NG, 1, 2 * BODIES + 1)


def layer1_start(nc, sems, e, b, N):
    q = sems("w1_", "iotas")
    with ExitStack() as ctx:
        order = ctx.enter_context(nc.sbuf_tensor("order", [TE, TE], I32))
        number = ctx.enter_context(nc.sbuf_tensor("number", [TE, 1], I32))
        with nc.Block() as block:
            @block.gpsimd
            def _(pool):
                pool.iota(order[:, :], [[-1, TE]], base=0, channel_multiplier=1).then_inc(q["iotas"], 1)
                pool.iota(number[:, :], [[0, 1]], base=N, channel_multiplier=1).then_inc(q["iotas"], 1)

            @block.vector
            def _(dve):
                dve.memset(e["pass_base"][:, :], -float(WIN))
                dve.wait_ge(q["iotas"], 2)
                dve.tensor_scalar(b["before"][:, :], order[:, :], 0.0, None, ALU.is_gt)
                dve.tensor_copy(b["spare"][:, :], number[:, :])


def layer1_pass(nc, a, d, s, e, b, T, N):
    BODIES = T // BT
    hot, same, window, turned, msg = b["hot"], b["same"], b["window"], b["turned"], b["msg"]
    turned_ps, msg_ps = b["turned_ps"], b["msg_ps"]
    src_rows_sem = [s["src_rows0"], s["src_rows1"]]
    rows = WIN * MAPS
    LAG = 2

    with nc.Block() as block:
        @block.sync
        def _(sp):
            sp.wait_ge(s["based"], 4)

            def load_sources(i, g):
                sp.wait_ge(s["idx_set"], 2 * i + g + 1)
                sp.dma_start(b["src_rows"][:, g, :, :].rearrange("p t e -> p (t e)"),
                             a["src"].rearrange("(o e) -> o e", o=1)[:, ds((BT * i + G * g) * TE, G * TE)]
                             .to_broadcast([TE, G * TE])).then_inc(src_rows_sem[g], 16)

            def load_windows(i, g):
                group_base = sp.value_load(e["group_base_i"][0:1, ds(2 * i + g + 1, 1)], min_val=0, max_val=N)
                packed = sp.value_load(e["packed_off"][0:1, ds(2 * i + g, 1)])
                for t in range(G * g, G * g + G):
                    base = nc.s_assert_within(group_base + packed // 64 ** (t % G) % 64, 0, N)
                    sp.wait_ge(s["msg_mm"], BT * i + t + 1)
                    sp.dma_start(window[:, t, :], d["maps1"][ds(base, WIN), :, :].rearrange("n k f -> (n k) f")) \
                        .then_inc(s["window"][t], 16)

            def body(i, more):
                load_sources(i, 1)
                load_windows(i, 0)
                if more:
                    load_sources(i + 1, 0)
                load_windows(i, 1)

            load_sources(0, 0)
            if BODIES > 1:
                with sp.Fori(0, BODIES - 1) as i:
                    body(i, True)
            body(BODIES - 1, False)

        @block.vector
        def _(dve):
            chain = Chain(dve, s["based"])
            dve.sem_inc(s["turned"], BT)
            dve.sem_inc(s["idx_set"], 2)
            set_windows(dve, chain, s, e, T // G)
            chain.wait()
            with dve.Fori(0, BODIES) as i:
                ch = Chain(dve, s["chain"], 10 * i)
                for g in range(2):
                    src = e["src_i"][:, ds(BT * i + G * g, G)]
                    dve.wait_ge(src_rows_sem[g], 16 * i + 16)
                    dve.wait_ge(s["turned"], BT * i + G * g + G)
                    ch.step(dve.tensor_tensor(same[:, g, :, :], b["src_rows"][:, g, :, :], spread(src, 2, TE),
                                              ALU.is_equal))
                    make_onehots(dve, ch, s, s["turned"], e, hot[:, :, :, :, :].rearrange("p g t n k -> p g t k n"), i, g)
                    ch.wait()
                    ch.step(dve.tensor_tensor(b["earlier"][:, :, :], same[:, g, :, :], spread(b["before"][:, :], 1, G),
                                              ALU.mult))
                    ch.wait()
                    ch.step(dve.tensor_reduce(b["double"][:, :], b["earlier"][:, :, :], AX.X, ALU.max))
                    ch.wait()
                    ch.step(dve.scalar_tensor_tensor(b["shift"][:, :], src, b["spare"][:, :], b["double"][:, :],
                                                     ALU.subtract, ALU.mult))
                    ch.wait()
                    for k in range(G):
                        dve.wait_ge(s["gathered"][G * g + k], 16 * i)
                    dve.tensor_tensor(e["idx_now"][:, g, :], src, b["shift"][:, :], ALU.subtract) \
                        .then_inc(s["idx_set"], 1)

        @block.tensor
        def _(pe):
            def turn(i, t):
                g, k = t // G, t % G
                if k == 0:
                    pe.wait_ge(s["onehots"], 2 * i + g + 1)
                pe.wait_ge(s["turned_out"], BT * i + t + 1)
                pe.matmul(turned_ps[0:rows, t % 2, 0:TE], hot[:, g, k, :, :].rearrange("p n k -> p (n k)"),
                          same[:, g, k, :], start=True, stop=True).then_inc(s["turned"], 1)

            def messages(i, t):
                pe.wait_ge(s["turned_out"], BT * i + t + 3)
                pe.wait_ge(s["window"][t], 16 * i + 16)
                pe.wait_ge(s["msg_out"], BT * i + t + 1)
                pe.matmul(msg_ps[0:TE, t % MSG_BANKS, 0:C], turned[:, t % 2, :], window[:, t, :], start=True, stop=True) \
                    .then_inc(s["msg_mm"], 1)

            pe.sem_inc(s["msg_mm"], BT)
            with pe.Fori(0, BODIES) as i:
                for t in range(BT + LAG):
                    if t < BT:
                        turn(i, t)
                    if t >= LAG:
                        messages(i, t - LAG)

        @block.scalar
        def _(act):
            def turned_rows(i, t):
                act.wait_ge(s["turned"], BT * i + t + 1 + BT)
                act.wait_ge(s["msg_mm"], BT * i + t - 1 + BT)
                act.activation(turned[:, t % 2, :], turned_ps[0:rows, t % 2, 0:TE], ACT.Copy) \
                    .then_inc(s["turned_out"], 1)

            def message_rows(i, t):
                act.wait_ge(s["msg_mm"], BT * i + t + 1 + BT)
                act.wait_ge(s["gathered"][t], 16 * i)
                act.activation(msg[:, t, :], msg_ps[0:TE, t % MSG_BANKS, 0:C], ACT.Copy).then_inc(s["msg_out"], 1)

            act.sem_inc(s["turned_out"], 2)
            act.sem_inc(s["msg_out"], MSG_BANKS)
            with act.Fori(0, BODIES) as i:
                for t in range(BT + LAG):
                    if t < BT:
                        turned_rows(i, t)
                    if t >= LAG:
                        message_rows(i, t - LAG)

        @block.gpsimd
        def _(pool):
            with pool.Fori(0, BODIES) as i:
                for t in range(BT):
                    g, k = t // G, t % G
                    if k == 0:
                        pool.wait_ge(s["idx_set"], 2 * i + g + 3)
                    pool.wait_ge(s["msg_out"], BT * i + t + 1 + MSG_BANKS)
                    if t < TABLES:
                        pool.wait_ge(s["gathered"][t + TABLES], 16 * i)
                    else:
                        pool.wait_ge(s["gathered"][t - TABLES], 16 * i + 16)
                    pool.sem_inc(s["mark"], 1)
                    pool.indirect_dma_start(d["sums1"][t % TABLES][:, :],
                                            bass.IndirectOffsetOnAxis(ap=e["idx_now"][:, g, k:k + 1], axis=0),
                                            msg[:, t, :], None, compute_op=ALU.add) \
                        .then_inc(s["gathered"][t], 16)
            end_of_pool_dmas(pool, s, T)


def middle_stage(nc, a, d, sb_in, ps_in, sems, ident, ident_b, agg_t, N):
    q = sems("mid_", "mark loaded0 loaded1 weights chain copied back pre sig gated var std normed h casts rests kept turned "
                     "h_t lin added turned_b parts stored0 stored1 mapped maps_stored0 maps_stored1")
    BODY_BLOCKS = 2 * CB
    BODIES = N // (TE * BODY_BLOCKS)
    CN = CB * TE
    with ExitStack() as ctx:
        x, x1 = sb_in(ctx, "x_mid", [TE, 2, CB, C]), sb_in(ctx, "x1", [TE, 2, CB, C])
        own, pre = sb_in(ctx, "own", [TE, 2, CB, PRE]), sb_in(ctx, "pre", [TE, CB, PRE])
        sig, agg_c = sb_in(ctx, "sig", [TE, CB, 96]), sb_in(ctx, "agg_c", [96, 2, 2, CN])
        t = dict(mean=sb_in(ctx, "mean1", [TE, CB]), var=sb_in(ctx, "var1", [TE, CB]), std=sb_in(ctx, "std1", [TE, CB]),
                 inv=sb_in(ctx, "inv1", [TE, CB]), centred=sb_in(ctx, "centred1", [TE, CB, C]),
                 square=sb_in(ctx, "square1", [TE, CB, C]))
        normed, h = sb_in(ctx, "normed1", [TE, CB, C]), sb_in(ctx, "h1", [TE, 2, CB, C])
        kept, rest = sb_in(ctx, "kept", [TE, 2, CB, C]), sb_in(ctx, "rest", [TE, CB, C])
        parts = sb_in(ctx, "parts", [TE, 2, CB, 5, 3, V], BF16)
        parts_c = sb_in(ctx, "parts_c", [96, 2, 5, CN], BF16)
        hs_t, hv_t = sb_in(ctx, "hs_t", [S, 2, CN]), sb_in(ctx, "hv_t", [96, 2, TE])
        node_w, m_s, m_v = sb_in(ctx, "node_w1", [TE, N // TE]), sb_in(ctx, "m_s", [S, 224]), sb_in(ctx, "m_v", [96, 480])
        maps = sb_in(ctx, "maps", [TE, 2, MAPS * C])
        back, turned = ps_in(ctx, "back", [128, 512]), ps_in(ctx, "turned1", [128, 2, 4, TE + 3])
        lin_a, lin_b = ps_in(ctx, "lin_a", [128, 2, 512]), ps_in(ctx, "lin_b", [128, 2, 512])
        turned_b = ps_in(ctx, "turned_b", [128, 8, TE + 3], BF16)
        maps_stored = [q["maps_stored0"], q["maps_stored1"]]
        loaded, stored = [q["loaded0"], q["loaded1"]], [q["stored0"], q["stored1"]]

        def chunk_of(ap, k):
            return node_blocks(ap)[:, ds(k, 1), :, :].rearrange("p k b f -> p (k b) f")

        with nc.Block() as block:
            @block.sync
            def _(sp):
                sp.dma_start(node_w[:, :], a["node_t"]).then_inc(q["weights"], 16)
                sp.dma_start(m_s[:, :], a["m_s"]).then_inc(q["weights"], 16)
                sp.dma_start(m_v[:, :], a["m_v"]).then_inc(q["weights"], 16)

                def load(k, par):
                    sp.dma_start(x[:, par, :, :], chunk_of(a["x"], k)).then_inc(loaded[par], 16)
                    sp.dma_start(own[:, par, :, :], chunk_of(d["own0"], k)).then_inc(loaded[par], 16)

                def store(k, i, par):
                    sp.wait_ge(q["added"], CB * (2 * i + par + 1))
                    sp.wait_ge(q["parts"], CB * (2 * i + par + 1))
                    sp.wait_ge(q["h_t"], CB * (2 * i + par + 1))
                    sp.dma_start(chunk_of(d["h1"], k), h[:, par, :, :]).then_inc(stored[par], 16)
                    sp.dma_start(chunk_of(d["kept1"], k), kept[:, par, :, :]).then_inc(stored[par], 16)
                    sp.dma_start(d["scalars1_t"][:, ds(k * CN, CN)], hs_t[:, par, :]).then_inc(stored[par], 16)
                    sp.dma_start(d["parts_t"][:, :, ds(k * CN, CN)], parts_c[:, par, :, :]).then_inc(stored[par], 16)

                load(0, 0)
                load(1, 1)
                if BODIES > 1:
                    with sp.Fori(0, BODIES - 1) as i:
                        for par in range(2):
                            store(2 * i + par, i, par)
                            load(2 * i + 2 + par, par)
                for par in range(2):
                    store(2 * BODIES - 2 + par, BODIES - 1, par)
                for par in range(2):
                    sp.wait_ge(stored[par], 64 * BODIES)

            @block.gpsimd
            def _(pool):
                with pool.Fori(0, BODIES) as i:
                    for par in range(2):
                        pool.wait_ge(q["back"], BODY_BLOCKS * i)
                        pool.sem_inc(q["mark"], 1)
                        pool.tensor_copy(agg_c[:, par, :, :], agg_t[:, :, ds((2 * i + par) * CN, CN)]) \
                            .then_inc(q["copied"], 1)
                    for par in range(2):
                        c = 2 * i + par
                        pool.wait_ge(q["h"], c + 1)
                        pool.wait_ge(stored[par], 64 * i)
                        pool.sem_inc(q["mark"], 1)
                        pool.tensor_tensor(kept[:, par, :, :], x1[:, par, :, :], h[:, par, :, :], ALU.add) \
                            .then_inc(q["kept"], 1)
                        by_part = parts[:, par, :, :, :, :].rearrange("p b g a c -> p (b g) a c")
                        h_g = h[:, par, :, :].rearrange("p b (g c) -> p (b g) c", c=V)
                        rest_g = rest[:, :, :].rearrange("p b (g c) -> p (b g) c", c=V)
                        for n in range(2):
                            pool.wait_ge(q["casts"], 3 * c + n + 1)
                            pool.wait_ge(q["rests"], 2 * c + n)
                            pool.sem_inc(q["mark"], 1)
                            pool.tensor_tensor(rest_g, h_g if n == 0 else rest_g, by_part[:, :, n, :], ALU.subtract) \
                            .then_inc(q["rests"], 1)

            @block.vector
            def _(dve):
                dve.wait_ge(q["weights"], 48)
                dve.memset(maps[:, :, :], 0.0)
                dve.tensor_scalar(m_s[:, :], m_s[:, :], INV8, None, ALU.mult)
                dve.tensor_scalar(m_v[:, 0:192], m_v[:, 0:192], INV_SQRT32 * INV_SQRT3, None, ALU.mult)
                dve.tensor_scalar(m_v[:, 192:480], m_v[:, 192:480], INV_SQRT32, None, ALU.mult).then_inc(q["gated"], 1)
                with dve.Fori(0, BODIES) as i:
                    chain = Chain(dve, q["chain"], 16 * i)
                    for par in range(2):
                        c = 2 * i + par
                        dve.wait_ge(loaded[par], 32 * i + 32)
                        dve.wait_ge(q["sig"], c)
                        for j in range(CB):
                            k = BODY_BLOCKS * i + CB * par + j
                            dve.wait_ge(q["back"], k + 1)
                            dve.scalar_tensor_tensor(pre[:, j, :], back[0:TE, 0:PRE],
                                                     node_w[:, ds(k, 1)], own[:, par, j, :], ALU.mult, ALU.add) \
                            .then_inc(q["pre"], 1)
                        dve.wait_ge(q["sig"], c + 1)
                        dve.wait_ge(q["pre"], BODY_BLOCKS * i + CB * par + CB)
                        dve.wait_ge(q["kept"], 2 * i)
                        vec = pre[:, :, 96:PRE].rearrange("p b (i c) -> p b i c", i=3)
                        dve.tensor_tensor(pre[:, :, 0:S], pre[:, :, 0:S], sig[:, :, 0:S], ALU.mult)
                        chain.step(dve.tensor_tensor(vec, vec, spread(sig[:, :, S:96], 2, 3), ALU.mult))
                        chain.wait()
                        dve.tensor_tensor(x1[:, par, :, 0:S], x[:, par, :, 0:S], pre[:, :, 0:S], ALU.add)
                        chain.step(dve.tensor_tensor(
                            x1[:, par, :, S:C].rearrange("p b (i c) -> p b i c", i=3), by_component(x[:, par, :, S:C]),
                            vec, ALU.add))
                        dve.wait_ge(q["h"], c)
                        last = normalise(dve, chain, q["var"], q["std"], c + 1, x1[:, par, :, :], t,
                                         t["centred"][:, :, 0:S],
                                         t["centred"][:, :, S:C].rearrange("p b (i c) -> p b i c", i=3),
                                         normed[:, :, :])
                        last.then_inc(q["normed"], 1)
                    for j in range(BODY_BLOCKS):
                        par, b, k = j // CB, j % CB, BODY_BLOCKS * i + j
                        if b == 0:
                            dve.wait_ge(stored[par], 64 * i)
                            dve.wait_ge(q["kept"], 2 * i + par + 1)
                        dve.wait_ge(q["turned_b"], k + 1)
                        dve.tensor_copy(parts_c[:, par, :, TE * b:TE * b + TE], turned_b[0:96, 0:5, 0:TE]) \
                            .then_inc(q["parts"], 1)
                        dve.wait_ge(q["lin"], k + 1)
                        dve.tensor_tensor(kept[:, par, b, :], kept[:, par, b, :], lin_b[0:TE, j % 2, 192:352], ALU.add)
                        dve.wait_ge(maps_stored[j % 2], 16 * (CB * i + j // 2))
                        dve.tensor_copy(maps[:, j % 2, :].rearrange("p (k f) -> p k f", f=C)[:, 0:5:4, S:C],
                                        lin_b[0:TE, j % 2, 0:192].rearrange("p (k f) -> p k f", k=2)) \
                            .then_inc(q["added"], 1)

            @block.scalar
            def _(act):
                def turned_features(i, j):
                    par, b, k = j // CB, j % CB, BODY_BLOCKS * i + j
                    act.wait_ge(q["turned"], k + 1)
                    act.wait_ge(q["lin"], k - 1 if j >= 2 else BODY_BLOCKS * i)
                    act.activation(hs_t[:, par, TE * b:TE * b + TE], turned[0:S, j % 2, 0, 0:TE], ACT.Copy)
                    act.activation(hv_t[:, j % 2, :], turned[0:96, j % 2, 1, 0:TE], ACT.Copy).then_inc(q["h_t"], 1)

                with act.Fori(0, BODIES) as i:
                    for par in range(2):
                        c = 2 * i + par
                        act.wait_ge(q["pre"], CB * (c + 1))
                        act.wait_ge(q["normed"], c)
                        act.activation(sig[:, :, :], pre[:, :, 0:96], ACT.Sigmoid).then_inc(q["sig"], 1)
                        act.wait_ge(q["var"], c + 1)
                        act.activation(t["std"][:, :], t["var"][:, :], ACT.Sqrt).then_inc(q["std"], 1)
                        act.wait_ge(q["normed"], c + 1)
                        act.wait_ge(q["turned"], BODY_BLOCKS * i)
                        act.wait_ge(stored[par], 64 * i)
                        act.activation(h[:, par, :, :], normed[:, :, :], ACT.Relu).then_inc(q["h"], 1)
                        act.wait_ge(q["h"], c + 1)
                        act.wait_ge(q["turned_b"], BODY_BLOCKS * i)
                        by_part = parts[:, par, :, :, :, :].rearrange("p b g a c -> p (b g) a c")
                        h_g = h[:, par, :, :].rearrange("p b (g c) -> p (b g) c", c=V)
                        rest_g = rest[:, :, :].rearrange("p b (g c) -> p (b g) c", c=V)
                        for n in range(3):
                            act.wait_ge(q["rests"], 2 * c + n)
                            act.activation(by_part[:, :, n, :], h_g if n == 0 else rest_g, ACT.Copy) \
                            .then_inc(q["casts"], 1)
                    turned_features(i, 0)
                    for j in range(BODY_BLOCKS):
                        par, b, k = j // CB, j % CB, BODY_BLOCKS * i + j
                        if j + 1 < BODY_BLOCKS:
                            turned_features(i, j + 1)
                        act.wait_ge(q["lin"], k + 1)
                        act.wait_ge(maps_stored[j % 2], 16 * (CB * i + j // 2))
                        by_map = maps[:, j % 2, :].rearrange("p (k f) -> p k f", f=C)
                        lin = lin_a[0:TE, j % 2, :]
                        act.activation(by_map[:, 0:5:4, 0:S], lin[:, 0:2 * S].rearrange("p (k f) -> p k f", k=2), ACT.Copy)
                        act.activation(maps[:, j % 2, C + S:C + S + 3 * (C + V)]
                                       .rearrange("p (k f) -> p k f", f=C + V)[:, :, 0:V],
                                       spread(lin[:, 2 * S:2 * S + V], 1, 3), ACT.Copy)
                        act.activation(by_map[:, 1:4, 0:S], lin[:, 160:352].rearrange("p (k f) -> p k f", k=3), ACT.Copy) \
                            .then_inc(q["mapped"], 1)
                        act.wait_ge(q["mapped"], k + 1)
                        act.wait_ge(q["added"], k + 1)
                        act.dma_start(d["maps1"][ds(k * TE, TE), :, :].rearrange("p k f -> p (k f)"), maps[:, j % 2, :]) \
                            .then_inc(maps_stored[j % 2], 16)
                for par in range(2):
                    act.wait_ge(maps_stored[par], 16 * CB * BODIES)

            @block.tensor
            def _(pe):
                pe.wait_ge(q["gated"], 1)

                def transposes(i, j):
                    par, b, k = j // CB, j % CB, BODY_BLOCKS * i + j
                    if b == 0:
                        pe.wait_ge(q["casts"], 3 * (2 * i + par) + 3)
                    pe.transpose(turned[0:96, j % 2, 1, 0:TE], h[:, par, b, S:C], ident[0:TE, 0:TE])
                    pe.transpose(turned[0:S, j % 2, 0, 0:TE], h[:, par, b, 0:S], ident[0:TE, 0:TE]) \
                        .then_inc(q["turned"], 1)
                    pe.wait_ge(q["parts"], k)
                    for g in range(5):
                        mm = pe.transpose(turned_b[0:96, g, 0:TE],
                                          parts[:, par, b, g, :, :].rearrange("p a c -> p (a c)"),
                                          ident_b[0:TE, 0:TE])
                    mm.then_inc(q["turned_b"], 1)

                def products(i, j):
                    par, b, k = j // CB, j % CB, BODY_BLOCKS * i + j
                    pe.wait_ge(q["h_t"], k + 1)
                    pe.wait_ge(q["added"], k - 1 if j >= 2 else BODY_BLOCKS * i)
                    pe.wait_ge(q["mapped"], k - 1 if j >= 2 else BODY_BLOCKS * i)
                    hs, hv = hs_t[:, par, TE * b:TE * b + TE], hv_t[:, j % 2, :]
                    for out, left, right in (
                            (lin_a[0:TE, j % 2, 0:160], hs, m_s[:, 0:160]),
                            (lin_b[0:TE, j % 2, 192:256], hs, m_s[:, 160:224]),
                            (lin_a[0:TE, j % 2, 160:352], hv, m_v[:, 0:192]),
                            (lin_b[0:TE, j % 2, 0:192], hv, m_v[:, 192:384]),
                            (lin_b[0:TE, j % 2, 256:352], hv, m_v[:, 384:480])):
                        mm = pe.matmul(out, left, right, start=True, stop=True)
                    mm.then_inc(q["lin"], 1)

                with pe.Fori(0, BODIES) as i:
                    for j in range(BODY_BLOCKS):
                        par, b, k = j // CB, j % CB, BODY_BLOCKS * i + j
                        if b == 0:
                            pe.wait_ge(q["copied"], 2 * i + par + 1)
                        pe.wait_ge(q["pre"], k)
                        for part in range(2):
                            mm = pe.transpose(back[0:TE, 96 * part:96 * part + 96],
                                              agg_c[:, par, part, TE * b:TE * b + TE], ident[0:96, 0:96])
                        mm.then_inc(q["back"], 1)
                    transposes(i, 0)
                    for j in range(BODY_BLOCKS):
                        if j + 1 < BODY_BLOCKS:
                            transposes(i, j + 1)
                        products(i, j)


def update_stage(nc, a, d, sb_in, ps_in, sems, zeros_b, ident, N):
    q = sems("upd_", "mark pe_mark loaded0 loaded1 weights iotas scaled chain a_wide turned a_t m rep prod "
                     "pair_done total_t total terms halved reduced summed out stored0 stored1")
    CHUNKS, PAIR = N // NC, 2 * NC
    SS_OPS, VV_OPS = 16, 12
    OPS = SS_OPS + VV_OPS
    TERMS_AT, REDUCE_AT = ((0, 2, 4, 6, 8, 10), (16, 17, 19, 20, 22, 23)), ((7, 11, 14), (21, 25, 27))
    with ExitStack() as ctx:
        w_ss, w_vv = sb_in(ctx, "w_ss", [128, 32, S]), sb_in(ctx, "w_vv", [128, 8, S])
        w_sv, w_vs = sb_in(ctx, "w_sv", [S, V * V]), sb_in(ctx, "w_vs", [S, V * V])
        sel_i = sb_in(ctx, "sel_i", [96, 16 * 128], I32)
        sel_s, sel_v = sb_in(ctx, "sel_s", [96, 16, 128], BF16), sb_in(ctx, "sel_v", [96, 8, 128], BF16)
        parts = sb_in(ctx, "parts_in", [96, 2, 5, NC], BF16)
        h_node, kept = sb_in(ctx, "h_node", [TE, 2, 2, C]), sb_in(ctx, "kept_in", [TE, 2, 2, C])
        hs_t = sb_in(ctx, "hs_t_in", [S, 2, NC])
        a_s = sb_in(ctx, "a_s", [128, 2, NC])
        a_v = sb_in(ctx, "a_v", [128, 2, 3, NC])
        sums = sb_in(ctx, "sums_in", [TE, 2, TABLES, 2, C])
        a_wide = sb_in(ctx, "a_wide", [TE, 2, 2, 2 * S + 12 * V])
        prod = sb_in(ctx, "prod", [128, 3, 2, NC])
        terms = sb_in(ctx, "terms", [TE, 3, V, 2, V])
        half = sb_in(ctx, "half", [TE, 3 * V, V])
        total_t = sb_in(ctx, "total_t", [S, NC])
        vec = sb_in(ctx, "vec", [TE, 2, 96])
        result = sb_in(ctx, "result", [TE, 2, 2, C])
        m_ps = ps_in(ctx, "m_ps", [128, 2, V * V])
        rep = ps_in(ctx, "rep", [128, 2, 512])
        total, turned = ps_in(ctx, "total", [128, 512]), ps_in(ctx, "turned2", [128, 512])
        loaded, stored = [q["loaded0"], q["loaded1"]], [q["stored0"], q["stored1"]]

        LOADS = 16 * (4 + TABLES)

        def turn(c, par):
            return c // 2 if isinstance(c, int) else (c - par) // 2

        def rows(ap, c):
            return ap.rearrange("(k b p) f -> p k b f", b=2, p=TE)[:, ds(c, 1), :, :] \
                .rearrange("p k b f -> p (k b) f")

        def chunks(engine, body):
            with engine.Fori(0, CHUNKS // 2) as i:
                body(2 * i, 0, (2 * i + 1, 1))
                body(2 * i + 1, 1, (2 * i + 2, 0))
            body(CHUNKS - 1, 0, None)

        def source(o):
            if o < SS_OPS:
                plane, first = o // 8, 2 * (o % 8)
                return plane, sel_s, first, None, w_ss, 2 * o
            i, first = divmod(o - SS_OPS, 4)
            return 2 + i, sel_v, 2 * first, i, w_vv, 2 * first

        with nc.Block() as block:
            @block.sync
            def _(sp):
                sp.dma_start(w_ss[:, :, :], a["wu_ss"].rearrange("(c j) v w -> (j v) c w", j=2)).then_inc(q["weights"], 16)
                sp.dma_start(w_vv[:, :, :], a["wu_vv"].rearrange("(c j) v w -> (j v) c w", j=4)).then_inc(q["weights"], 16)
                sp.dma_start(w_sv[:, :], a["wu_sv"]).then_inc(q["weights"], 16)
                sp.dma_start(w_vs[:, :], a["wu_vs"]).then_inc(q["weights"], 16)

                def load(c, par):
                    sp.dma_start(parts[:, par, :, :], d["parts_t"][:, :, ds(c * NC, NC)]).then_inc(loaded[par], 16)
                    sp.dma_start(h_node[:, par, :, :], rows(d["h1"], c)).then_inc(loaded[par], 16)
                    for k in range(TABLES):
                        sp.dma_start(sums[:, par, k, :, :], rows(d["sums1"][k][0:N, :], c)).then_inc(loaded[par], 16)
                    sp.dma_start(kept[:, par, :, :], rows(d["kept1"], c)).then_inc(loaded[par], 16)
                    sp.dma_start(hs_t[:, par, :], d["scalars1_t"][:, ds(c * NC, NC)]).then_inc(loaded[par], 16)

                def store(c, par):
                    sp.wait_ge(q["out"], c + 1)
                    sp.dma_start(rows(a["out"], c), result[:, par, :, :]).then_inc(stored[par], 16)

                load(0, 0)
                load(1, 1)
                if CHUNKS > 3:
                    with sp.Fori(0, CHUNKS // 2 - 1) as i:
                        for par in range(2):
                            store(2 * i + par, par)
                            load(2 * i + 2 + par, par)
                store(CHUNKS - 3, 0)
                load(CHUNKS - 1, 0)
                store(CHUNKS - 2, 1)
                store(CHUNKS - 1, 0)
                sp.wait_ge(stored[0], 16 * (CHUNKS - CHUNKS // 2))
                sp.wait_ge(stored[1], 16 * (CHUNKS // 2))

            @block.gpsimd
            def _(pool):
                for part in range(3):
                    pool.iota(sel_i[V * part:V * part + V, :], [[-2, 16], [-1, 2], [0, 64]], base=0,
                              channel_multiplier=1).then_inc(q["iotas"], 1)
                pool.wait_ge(q["scaled"], 1)
                for part in range(3):
                    pool.iota(sel_i[V * part:V * part + V, 0:8 * 128], [[-4, 8], [-1, 4], [0, 32]], base=0,
                              channel_multiplier=1).then_inc(q["iotas"], 1)
                pool.wait_ge(q["iotas"], 6)

                def halve(c, blk):
                    for i in range(3):
                        n = 6 * c + 3 * blk + i
                        pool.wait_ge(q["terms"], n + 1)
                        pool.wait_ge(q["reduced"], n + 1)
                        pool.sem_inc(q["mark"], 1)
                        pool.tensor_tensor(half[:, V * i:V * i + V, :], terms[:, i, :, 0, :], terms[:, i, :, 1, :],
                                           ALU.add).then_inc(q["halved"], 1)

                def add_tables(c, par):
                    pool.wait_ge(loaded[par], LOADS * turn(c, par) + LOADS)
                    for k in range(1, TABLES):
                        pool.wait_ge(q["chain"], (TABLES - 1) * c + k - 1)
                        pool.sem_inc(q["mark"], 1)
                        pool.tensor_tensor(sums[:, par, 0, :, :], sums[:, par, 0, :, :], sums[:, par, k, :, :], ALU.add) \
                            .then_inc(q["chain"], 1)

                def chunk(c, par, following):
                    halve(c, 0)
                    if following:
                        add_tables(*following)
                    halve(c, 1)

                pool.sem_inc(q["halved"], 3)
                add_tables(0, 0)
                chunks(pool, chunk)

            @block.scalar
            def _(act):
                def copies(c, par):
                    act.wait_ge(q["chain"], (TABLES - 1) * (c + 1))
                    act.activation(a_wide[:, par, :, 0:2 * S].rearrange("p b (r f) -> p b r f", r=2),
                                   spread(sums[:, par, 0, :, 0:S], 2, 2), ACT.Copy)
                    for blk in range(2):
                        last = act.activation(
                            a_wide[:, par, blk, 2 * S:].rearrange("p (i r f) -> p i r f", i=3, r=4),
                            spread(sums[:, par, 0, blk, S:C].rearrange("p (i f) -> p i f", i=3), 2, 4), ACT.Copy)
                    last.then_inc(q["a_wide"], 1)
                    act.wait_ge(q["turned"], 2 * c + 1)
                    act.activation(a_s[:, par, :], turned[:, 0:NC], ACT.Copy)
                    act.activation(a_v[:, par, 0, :], turned[:, NC:2 * NC], ACT.Copy).then_inc(q["a_t"], 1)
                    act.wait_ge(q["turned"], 2 * c + 2)
                    act.activation(a_v[:, par, 1:3, :], turned[:, 0:2 * NC].rearrange("p (k n) -> p k n", k=2),
                                   ACT.Copy).then_inc(q["a_t"], 1)

                def chunk(c, par, following):
                    if following:
                        act.wait_ge(q["out"], c)
                        copies(*following)
                    act.wait_ge(q["pair_done"], OPS * (c + 1))
                    act.activation(total_t[:, :], total[0:S, 0:NC], ACT.Copy).then_inc(q["total_t"], 1)

                copies(0, 0)
                chunks(act, chunk)

            @block.tensor
            def _(pe):
                pe.wait_ge(q["scaled"], 6)

                def matrices(c, par, blk, piece):
                    if piece == 0:
                        pe.wait_ge(q["terms"], 6 * c + 3 * blk)
                    n, f = piece // 2, 512 * (piece % 2)
                    left, right = ((hs_t[:, par], w_sv), (a_s[0:S, par], w_vs))[n]
                    mm = pe.matmul(m_ps[0:TE, n, f:f + 512], left[:, TE * blk:TE * blk + TE], right[:, f:f + 512],
                                   start=True, stop=True)
                    if piece == 3:
                        mm.then_inc(q["m"], 1)

                def turn_sums(c, par, pair):
                    if pair == 0:
                        pe.wait_ge(loaded[par], LOADS * turn(c, par) + LOADS)
                        pe.wait_ge(q["a_wide"], c + 1)
                    pe.wait_ge(q["a_t"], 2 * c + pair)
                    for k in range(2):
                        for blk in range(2):
                            first = 128 * (2 * pair + k)
                            mm = pe.transpose(turned[:, NC * k + TE * blk:NC * k + TE * blk + TE],
                                              a_wide[:, par, blk, first:first + 128], ident[0:TE, 0:TE])
                    mm.then_inc(q["turned"], 1)

                def copy_rows(c, par, o):
                    plane, sel, first, _, _, _ = source(o)
                    pe.wait_ge(q["prod"], OPS * c + o - 1 if o >= 2 else OPS * c)
                    for t in range(2):
                        mm = pe.matmul(rep[:, o % 2, NC * t:NC * t + NC], sel[:, first + t, :], parts[:, par, plane, :],
                                       start=True, stop=True)
                    mm.then_inc(q["rep"], 1)

                def contract(c, o):
                    _, _, _, _, weight, first = source(o)
                    pe.wait_ge(q["prod"], OPS * c + o + 1)
                    for t in range(2):
                        mm = pe.matmul(total[0:S, 0:NC], weight[:, first + t, :], prod[:, o % 3, t, :],
                                       start=(o == 0 and t == 0), stop=(o == OPS - 1 and t == 1))
                    mm.then_inc(q["pair_done"], 1)

                def chunk(c, par, following):
                    pe.wait_ge(q["summed"], c)
                    for o in range(OPS):
                        contract(c, o)
                        if o + 2 < OPS:
                            copy_rows(c, par, o + 2)
                        if 11 <= o < 15:
                            matrices(c, par, 1, o - 11)
                        if following:
                            if o in (16, 18):
                                turn_sums(*following, (o - 16) // 2)
                            if o == OPS - 4:
                                pe.wait_ge(q["a_t"], 2 * c + 3)
                            if o >= OPS - 4:
                                matrices(*following, 0, o - OPS + 4)
                    if following:
                        copy_rows(*following, 0)
                        copy_rows(*following, 1)
                    pe.wait_ge(q["total_t"], c + 1)
                    pe.sem_inc(q["pe_mark"], 1)
                    for blk in range(2):
                        mm = pe.transpose(total[0:TE, NC + 6 + S * blk:NC + 6 + S * blk + S],
                                          total_t[:, TE * blk:TE * blk + TE], ident[0:S, 0:S])
                    mm.then_inc(q["total"], 1)

                for pair in range(2):
                    turn_sums(0, 0, pair)
                pe.wait_ge(q["a_t"], 1)
                for piece in range(4):
                    matrices(0, 0, 0, piece)
                copy_rows(0, 0, 0)
                copy_rows(0, 0, 1)
                chunks(pe, chunk)

            @block.vector
            def _(dve):
                dve.wait_ge(q["iotas"], 3)
                dve.tensor_scalar(sel_s[:, :, :].rearrange("p c n -> p (c n)"), sel_i[:, :], 0.0, None, ALU.is_equal) \
                    .then_inc(q["scaled"], 1)
                dve.wait_ge(q["iotas"], 6)
                dve.tensor_scalar(sel_v[:, :, :].rearrange("p c n -> p (c n)"), sel_i[:, 0:8 * 128], 0.0, None,
                                  ALU.is_equal).then_inc(q["scaled"], 1)
                dve.wait_ge(q["weights"], 64)
                for w, k in ((w_ss[:, :, :], INV64), (w_vv[:, :, :], INV_SQRT3 * INV32),
                             (w_sv[:, :], INV_SQRT2048), (w_vs[:, :], INV_SQRT2048)):
                    dve.tensor_scalar(w, w, k, None, ALU.mult).then_inc(q["scaled"], 1)

                def vector_terms(c, par, blk, piece):
                    i, n = divmod(piece, 2)
                    if piece == 0:
                        dve.wait_ge(q["m"], 2 * c + blk + 1)
                    dve.wait_ge(q["halved"], 6 * c + 3 * blk + i + 1)
                    source_i = (sums[:, par, 0] if n == 0 else h_node[:, par])[:, blk, S + V * i:S + V * i + V]
                    ins = dve.tensor_tensor(terms[:, i, :, n, :], m_ps[0:TE, n, :].rearrange("p (w v) -> p w v", v=V),
                                            spread(source_i, 1, V), ALU.mult)
                    if n == 1:
                        ins.then_inc(q["terms"], 1)

                def reduce(c, blk, i):
                    dve.wait_ge(q["halved"], 6 * c + 3 * blk + i + 4)
                    dve.tensor_reduce(vec[:, blk, V * i:V * i + V], half[:, V * i:V * i + V, :], AX.X, ALU.add) \
                        .then_inc(q["reduced"], 1)

                def product(c, par, o):
                    i = source(o)[3]
                    dve.wait_ge(q["rep"], OPS * c + o + 1)
                    dve.wait_ge(q["pair_done"], OPS * c + o - 2 if o >= 3 else OPS * c)
                    other = a_s[:, par, :] if i is None else a_v[:, par, i, :]
                    dve.tensor_tensor(prod[:, o % 3, :, :], rep[:, o % 2, 0:2 * NC].rearrange("p (t n) -> p t n", t=2),
                                      spread(other, 1, 2), ALU.mult).then_inc(q["prod"], 1)

                def chunk(c, par, following):
                    dve.wait_ge(loaded[par], LOADS * turn(c, par) + LOADS)
                    dve.wait_ge(q["a_t"], 2 * c + 2)
                    for o in range(OPS):
                        product(c, par, o)
                        for blk in range(2):
                            if o in TERMS_AT[blk]:
                                vector_terms(c, par, blk, TERMS_AT[blk].index(o))
                            if o in REDUCE_AT[blk]:
                                reduce(c, blk, REDUCE_AT[blk].index(o))
                    dve.wait_ge(q["total"], c + 1)
                    dve.wait_ge(stored[par], 16 * turn(c, par))
                    dve.tensor_tensor(result[:, par, :, 0:S], kept[:, par, :, 0:S],
                                      total[0:TE, NC + 6:NC + 6 + 2 * S].rearrange("p (b f) -> p b f", b=2), ALU.add) \
                        .then_inc(q["summed"], 1)
                    dve.wait_ge(q["reduced"], 6 * c + 9)
                    dve.tensor_tensor(by_component(result[:, par, :, S:C]),
                                      kept[:, par, :, S:C].rearrange("p b (i c) -> p b i c", i=3),
                                      vec[:, :, :].rearrange("p b (i c) -> p b i c", i=3), ALU.add) \
                        .then_inc(q["out"], 1)

                dve.sem_inc(q["reduced"], 3)
                chunks(dve, chunk)


def kernel(**inputs):
    import numpy as np
    import concourse.bacc as bacc
    from concourse.bass_utils import run_bass_kernel_spmd

    arrays = layout({k: np.asarray(v) for k, v in inputs.items()})
    nc = bacc.Bacc("TRN2", target_bir_lowering=False, num_devices=1)
    aps = {}
    for name, value in arrays.items():
        aps[name] = nc.dram_tensor("in_" + name, value.shape, mybir.dt.from_np(value.dtype), kind="ExternalInput").ap()
    aps["out"] = nc.dram_tensor("out", arrays["x"].shape, F32, kind="ExternalOutput").ap()
    build(nc, aps)
    r = run_bass_kernel_spmd(nc, [{"in_" + k: v for k, v in arrays.items()}], core_ids=[0])
    return r.results[0]["out"]


def layout(g):
    import numpy as np

    E, N = g["src"].shape[0], g["x"].shape[0]
    T = E // TE

    def f(shape):
        return np.zeros(shape, np.float32)

    def diagonal(*blocks):
        k, m = blocks[0].shape
        out = f((3 * k, 3 * m * len(blocks)))
        for n, w in enumerate(blocks):
            for i in range(3):
                out[k * i:k * i + k, m * (3 * n + i):m * (3 * n + i) + m] = w
        return out

    edge_t = f((128, (T // BT + 1) * (BT // 2) * TE))
    edge_t[:, :T // 2 * TE] = g["edge_attr_64"].reshape(T // 2, 2, TE, S).transpose(1, 3, 0, 2).reshape(2 * S, -1)
    fc1 = f((128, 128))
    fc1[:S, :S] = fc1[S:, S:] = g["L0_gnn_fc_w1"]
    w1, w2, w3, w4, w5 = np.split(g["L0_gnn_fc_w2"], [64, 128, 160, 192], axis=1)
    fc2 = f((128, 2, W5))
    fc2[:S, 0] = fc2[S:, 1] = np.concatenate([w2, w1, w4, w5, w3], axis=1)
    lin2_s = f((128, 96))
    lin2_s[:V], lin2_s[S:] = g["L0_gnn_lin2_ws"][S:], g["L0_gnn_lin2_ws"][:S]
    arrays = {
        "x": g["x"],
        "src_t": g["src"].reshape(T, TE).T, "dst_t": g["dst"].reshape(T, TE).T, "dst": g["dst"], "src": g["src"],
        "attr_t": g["edge_attr_4"].reshape(T, TE, 4).transpose(1, 0, 2),
        "edge_t": edge_t,
        "node_t": g["node_vec1"].reshape(N // TE, TE).T,
        "lin_s": np.concatenate([g["L0_gnn_lin1_ws"], g["L0_gnn_sc_ws"]], axis=1),
        "lin_v": diagonal(g["L0_gnn_lin1_wv"], g["L0_gnn_sc_wv"]),
        "fc1": fc1, "fc2": fc2,
        "lin2_s": lin2_s, "lin2_v": g["L0_gnn_lin2_wv"],
        "m_s": np.concatenate([g["L1_gnn_Lm_s"], g["L1_gnn_Wm_ss"], g["L1_gnn_Wm_sv"], g["L1_gnn_Lu_s"]], axis=1),
        "m_v": np.concatenate([diagonal(g["L1_gnn_Wm_vv"]),
                               diagonal(g["L1_gnn_Lm_v"], g["L1_gnn_Wm_vs"], g["L1_gnn_Lu_v"])], axis=1),
        "wu_ss": g["L1_gnn_Wu_ss"], "wu_vv": g["L1_gnn_Wu_vv"],
        "wu_sv": g["L1_gnn_Wu_sv"].transpose(0, 2, 1).reshape(S, V * V),
        "wu_vs": g["L1_gnn_Wu_vs"].transpose(1, 2, 0).reshape(S, V * V),
    }
    return {k: np.ascontiguousarray(v) for k, v in arrays.items()}
```
